# Optimizing a Trainium2 kernel written in Bass

```python
import numpy as np
import jax
import jax.numpy as jnp

def _softmax(x, axis=-1):
    return jax.nn.softmax(x, axis=axis)

def _gelu(x):
    return jax.nn.gelu(x, approximate=True)

def _silu(x):
    return jax.nn.silu(x)

def _sigmoid(x):
    return jax.nn.sigmoid(x)

def _layernorm(x, axis=-1, eps=1e-05):
    m = jnp.mean(x, axis=axis, keepdims=True)
    v = jnp.var(x, axis=axis, keepdims=True)
    return (x - m) / jnp.sqrt(v + eps)

def _scatter_add(tgt, idx, src, axis=0):
    return tgt.at[idx].add(src)

def _segment_sum(src, seg, n):
    return jax.ops.segment_sum(src, seg, n)
kernel_name = 'mk_flamingo_gated_d1_seqx_r8_e0e1d5'

def setup_inputs(seed: int=0):
    np.random.seed(seed)
    _w = jnp.asarray

    def _rec_inputs():
        import jax
        import jax.numpy as jnp
        _rk = jax.random.key(seed)
        x = -7.109e-05 + 0.9999 * jax.random.normal(jax.random.fold_in(_rk, 1), (32, 64, 512), jnp.float32)
        _lenS = 64 - jax.random.randint(jax.random.fold_in(_rk, 7), (32,), 0, max(1, 64 // 4) + 1, jnp.int32)
        _lenS2 = 64 - jax.random.randint(jax.random.fold_in(_rk, 8), (32,), 0, max(1, 64 // 4) + 1, jnp.int32)
        _ctx_4096P = jax.random.normal(jax.random.fold_in(_rk, 11), (32, 16, 512), jnp.float32)
        _ctx_4096c = jax.random.dirichlet(jax.random.fold_in(_rk, 511), 0.3 * jnp.ones((16,), jnp.float32), (32, 64))
        _ctx_4096t = jnp.einsum('bsk,bkd->bsd', _ctx_4096c, _ctx_4096P)
        _ctx_4096t = _ctx_4096t * jax.lax.rsqrt(jnp.mean(jnp.square(_ctx_4096t)) + 1e-12) * 0.953939
        ctx_4096 = -2.6191e-05 + 0.999952 * (_ctx_4096t + 0.3 * jax.random.normal(jax.random.fold_in(_rk, 611), (32, 64, 512), jnp.float32))
        _g = jax.random.normal(jax.random.fold_in(_rk, 9001), (2, 1), jnp.float32)
        _g = jnp.sign(_g) * jnp.maximum(jnp.abs(_g), 1.0) + (_g == 0) * 1.0
        g_xattn = _g[0]
        g_ffn = _g[1]
        return (x, ctx_4096, g_xattn, g_ffn)
    x, ctx_4096, g_xattn, g_ffn = _rec_inputs()

    def _L0_xattn_setup():
        import jax, jax.numpy as jnp
        import numpy as np
        TEXT_DIM = 512
        FEATURE_DIM = 512

        def _xavier_uniform(key, shape):
            fan_in, fan_out = (shape[1], shape[0])
            limit = float(np.sqrt(6.0 / (fan_in + fan_out)))
            return jax.random.uniform(key, shape, jnp.float32, -limit, limit)
        key = jax.random.key(seed)
        k1, k2, k3, k4 = jax.random.split(key, 4)
        text = jax.random.normal(k1, (8, 256, TEXT_DIM), jnp.float32)
        features = jax.random.normal(k2, (8, 72, FEATURE_DIM), jnp.float32)
        Wq = _xavier_uniform(k3, (FEATURE_DIM, TEXT_DIM))
        bq = jnp.zeros((FEATURE_DIM,), jnp.float32)
        Wk = _xavier_uniform(k4, (FEATURE_DIM, FEATURE_DIM))
        bk = jnp.zeros((FEATURE_DIM,), jnp.float32)
        return {'text': text, 'features': features, 'Wq': Wq, 'bq': bq, 'Wk': Wk, 'bk': bk}
    _L0_xattn_all = _L0_xattn_setup()
    _L0_xattn_in = {k: v for k, v in _L0_xattn_all.items() if k in ('Wq', 'bq', 'Wk', 'bk')}
    del _L0_xattn_all

    def _L0_ffn_setup():
        import jax, jax.numpy as jnp
        import numpy as np
        TOP_K = 2
        key = jax.random.key(seed)
        k0, k1, k2 = jax.random.split(key, 3)
        B, S, D, H, E = (4, 256, 512, 512, 8)
        sc = 1.0 / np.sqrt(D).astype(np.float32)
        x = jax.random.normal(k0, (B, S, D), dtype=jnp.float32)
        W_gate = jax.random.normal(k1, (D, E), dtype=jnp.float32) * sc
        b_gate = jnp.zeros((E,), dtype=jnp.float32)
        W_e = jax.random.normal(k2, (E, D, H), dtype=jnp.float32) * sc
        b_e = jnp.zeros((E, H), dtype=jnp.float32)
        return {'x': x, 'W_gate': W_gate, 'b_gate': b_gate, 'W_e': W_e, 'b_e': b_e}
    _L0_ffn_all = _L0_ffn_setup()
    _L0_ffn_in = {k: v for k, v in _L0_ffn_all.items() if k in ('W_gate', 'b_gate', 'W_e', 'b_e')}
    del _L0_ffn_all
    return {'x': x, 'ctx_4096': ctx_4096, 'g_xattn': g_xattn, 'g_ffn': g_ffn, 'L0_xattn_Wq': _L0_xattn_in['Wq'], 'L0_xattn_bq': _L0_xattn_in['bq'], 'L0_xattn_Wk': _L0_xattn_in['Wk'], 'L0_xattn_bk': _L0_xattn_in['bk'], 'L0_ffn_W_gate': _L0_ffn_in['W_gate'], 'L0_ffn_b_gate': _L0_ffn_in['b_gate'], 'L0_ffn_W_e': _L0_ffn_in['W_e'], 'L0_ffn_b_e': _L0_ffn_in['b_e']}

def reference(x, ctx_4096, g_xattn, g_ffn, L0_xattn_Wq, L0_xattn_bq, L0_xattn_Wk, L0_xattn_bk, L0_ffn_W_gate, L0_ffn_b_gate, L0_ffn_W_e, L0_ffn_b_e):
    import jax
    import jax.numpy as jnp

    def _L0_xattn_ref(text, features, Wq, bq, Wk, bk):
        import jax, jax.numpy as jnp
        import numpy as np
        TEXT_DIM = 512
        FEATURE_DIM = 512

        def _xavier_uniform(key, shape):
            fan_in, fan_out = (shape[1], shape[0])
            limit = float(np.sqrt(6.0 / (fan_in + fan_out)))
            return jax.random.uniform(key, shape, jnp.float32, -limit, limit)
        Q = jnp.einsum('btx,dx->btd', text, Wq) + bq
        K = jnp.einsum('bpx,dx->bpd', features, Wk) + bk
        scale = 1.0 / jnp.sqrt(jnp.asarray(K.shape[-1], K.dtype))
        scores = jnp.einsum('btd,bpd->btp', Q, K) * scale
        attn = jax.nn.softmax(scores, axis=-1)
        attended = jnp.einsum('btp,bpd->btd', attn, features)
        return attended

    def _L0_ffn_ref(x, W_gate, b_gate, W_e, b_e):
        import jax, jax.numpy as jnp
        import numpy as np
        TOP_K = 2
        logits = x @ W_gate + b_gate
        _, top_idx = jax.lax.top_k(logits, TOP_K)
        y_all = jax.nn.relu(jnp.einsum('bsd,edh->bseh', x, W_e) + b_e)
        y = jnp.take_along_axis(y_all, top_idx[..., None], axis=2)
        return y.mean(axis=2)
    x = x + jnp.tanh(g_xattn[0]) * _L0_xattn_ref(_layernorm(x, axis=-1), ctx_4096, L0_xattn_Wq, L0_xattn_bq, L0_xattn_Wk, L0_xattn_bk)
    x = x + jnp.tanh(g_ffn[0]) * _L0_ffn_ref(_layernorm(x, axis=-1), L0_ffn_W_gate, L0_ffn_b_gate, L0_ffn_W_e, L0_ffn_b_e)
    return x

_drawn_inputs = setup_inputs


def setup_inputs(seed=0):
    import zlib

    import numpy as np

    out = dict(_drawn_inputs(seed))
    spreads = {'L0_xattn_bq': (0.0, 0.1),
     'L0_xattn_bk': (0.0, 0.1),
     'L0_ffn_b_gate': (0.0, 0.1),
     'L0_ffn_b_e': (0.0, 0.1)}
    factors = {}
    for name, (base, spread) in spreads.items():
        noise = np.random.default_rng([zlib.crc32(name.encode()), seed]).standard_normal(out[name].shape)
        drawn = base * np.exp(spread * noise) if base else spread * noise
        out[name] = jnp.asarray(drawn.astype(out[name].dtype))
    for name, factor in factors.items():
        out[name] = (out[name] * factor).astype(out[name].dtype)
    return out
```

```python
import concourse.bass as bass
from concourse import mybir
from contextlib import ExitStack

fp32 = mybir.dt.float32
fp32r = mybir.dt.float32r
fp16 = mybir.dt.float16
bf16 = mybir.dt.bfloat16
i32 = mybir.dt.int32
u32 = mybir.dt.uint32
ALU = mybir.AluOpType
ACT = mybir.ActivationFunctionType
AX = mybir.AxisListType
ds = bass.ds

P = 128
B, S, D = 32, 64, 512
E, TOPK = 8, 2
KC = D // P
N = B * S
TJ = 2
GT = TJ * P
GROUPS = N // GT
TILES = N // P
XR = 4
BLOCKS = (TOPK * N - E) // P + E
BU = 3
BW = BLOCKS + BLOCKS % 2
HALVES = 2 * E
HK = KC // 2
SCALE = float(D) ** -0.5
EPS = 1e-5
assert BLOCKS % BU == 0 and GROUPS % 2 == 0


def gated_xattn_moe(nc, x, ctx_, g_x, g_f, Wq, bq, Wk, bk, Wg, bg, We, be, out):
    x_v = x.rearrange("b s d -> (b s) d").rearrange("(g j p) d -> p g j d", j=TJ, p=P)
    c_v = ctx_.rearrange("b s d -> (b s) d").rearrange("(g j p) d -> p g j d", j=TJ, p=P)
    out_v = out[0:N, :].rearrange("(g j p) d -> p g j d", j=TJ, p=P)
    we_v = We.rearrange("e (k p) h -> p (e k) h", p=P)
    h_dram = nc.dram_tensor("h_dram", [N, D], fp32, kind="Internal").ap()
    h_v = h_dram.rearrange("(g j p) d -> p g j d", j=TJ, p=P)

    ctx = ExitStack()
    with ctx:
        def sb_in(stack, name, shape, dt):
            return stack.enter_context(nc.sbuf_tensor(name, shape, dt))

        def sem(name):
            return ctx.enter_context(nc.semaphore(name))

        def sb(name, shape, dt):
            return sb_in(ctx, name, shape, dt)

        we_hi = sb("we_hi", [P, E * KC, D], fp32r)
        we_lo = sb("we_lo", [P, E * KC, D], fp32r)
        ident = sb("ident", [P, P], fp32)
        earlier = sb("earlier", [P, P], bf16)
        ones_b = sb("ones_b", [P, P], bf16)
        ones8 = sb("ones8", [P, E], fp32)
        iota_e = sb("iota_e", [P, E], fp32)
        iota_p = sb("iota_p", [P, P], fp32)
        iota_blk = sb("iota_blk", [P, BW], fp32)
        token1 = sb("token1", [P, TILES], fp32)
        pad_row = sb("pad_row", [P, 1], fp32)
        half_neg = sb("half_neg", [P, TJ], fp32)
        gates = sb("gates", [P, 2], fp32)
        tanh_g = sb("tanh_g", [P, 2], fp32)
        ffn_gain = sb("ffn_gain", [P, 1], fp32)
        chosen = sb("chosen", [P, TOPK, TILES, E], fp32)
        rank = sb("rank", [P, TILES, E], fp32)
        taken = sb("taken", [P, E], bf16)
        slot_of = sb("slot_of", [P, TOPK, TILES], fp32)
        blk_of = sb("blk_of", [P, TOPK, TILES], fp32)
        gather_row = sb("gather_row", [P, BW], u32)
        add_row = sb("add_row", [P, BW], u32)
        gather_at = sb("gather_at", [P, BU], u32)
        gate = sb("gate", [1, 1], fp32)
        add_at = sb("add_at", [P, BU], u32)
        expert_of = sb("expert_of", [1, BW], i32)

        s1 = ExitStack()
        x_sb = sb_in(s1, "x_sb", [P, XR, TJ, D], fp32)
        s0 = ExitStack()
        wq_sb = sb_in(s0, "wq_sb", [P, KC, D], fp32)
        wk_sb = sb_in(s0, "wk_sb", [P, KC, D], fp32)
        bqk = sb_in(s0, "bqk", [P, 2, KC], fp32)
        bq_rows = sb_in(s0, "bq_rows", [P, KC, P], fp32)
        s0.close()
        aT_hi = sb_in(s1, "aT_hi", [P, KC, GT], fp32r)
        aT_lo = sb_in(s1, "aT_lo", [P, KC, GT], fp32r)
        gT = sb_in(s1, "gT", [P, KC, GT], fp32)
        cT = sb_in(s1, "cT", [P, TJ, KC, P], fp32)
        hT = sb_in(s1, "hT", [P, TJ, KC, P], fp32)
        c_sb = sb_in(s1, "c_sb", [P, 2, TJ, D], fp32)
        m_hi = sb_in(s1, "m_hi", [P, KC, D], fp32r)
        m_lo = sb_in(s1, "m_lo", [P, KC, D], fp32r)
        a_sb = sb_in(s1, "a_sb", [P, TJ, D], fp32)
        h_sb = sb_in(s1, "h_sb", [P, TJ, D], fp32)
        w_raw = sb_in(s1, "w_raw", [P, HK, D], fp32)
        wg_sb = sb_in(s1, "wg_sb", [P, KC, E], fp32)
        bg_sb = sb_in(s1, "bg_sb", [P, E], fp32)
        w_vec = sb_in(s1, "w_vec", [P, KC], fp32)
        u_vec = sb_in(s1, "u_vec", [P, KC, 2], fp32r)
        bb = sb_in(s1, "bb", [P, 1], fp32)
        s_sb = sb_in(s1, "s_sb", [P, TJ, S], fp32)
        p_sb = sb_in(s1, "p_sb", [P, TJ, P], fp32)
        pT_sb = sb_in(s1, "pT_sb", [P, TJ, P], fp32)
        row_sum = sb_in(s1, "row_sum", [P, TJ], fp32)
        row_term = sb_in(s1, "row_term", [P, TJ], fp32)
        peak = sb_in(s1, "peak", [P, TJ], fp32)
        neg_peak = sb_in(s1, "neg_peak", [P, TJ], fp32)
        exp_sum = sb_in(s1, "exp_sum", [P, TJ], fp32)
        exp_inv = sb_in(s1, "exp_inv", [P, TJ], fp32)
        att_gain = sb_in(s1, "att_gain", [P, TJ], fp32)
        st1 = sb_in(s1, "st1", [P, TJ, 6], fp32)
        mv1 = sb_in(s1, "mv1", [P, TJ, 2], fp32)
        ve1 = sb_in(s1, "ve1", [P, TJ], fp32)
        rstd1 = sb_in(s1, "rstd1", [P, TJ], fp32)
        st2 = sb_in(s1, "st2", [P, TJ, 6], fp32)
        mv2 = sb_in(s1, "mv2", [P, TJ, 2], fp32)
        ve2 = sb_in(s1, "ve2", [P, TJ], fp32)
        rstd2 = sb_in(s1, "rstd2", [P, TJ], fp32)
        logit = sb_in(s1, "logit", [P, TJ, E], fp32)
        best = sb_in(s1, "best", [P, TJ, E], fp32)
        best_at = sb_in(s1, "best_at", [P, TJ, E], u32)
        best_f = sb_in(s1, "best_f", [P, TJ, TOPK], fp32)
        mask = sb_in(s1, "mask", [P, TJ, E], bf16)
        s1.close()
        s2 = ExitStack()
        be_sb = sb_in(s2, "be_sb", [P, E, D], fp32)
        in_slot = sb_in(s2, "in_slot", [P, TOPK * TILES, P], fp16)
        in_blk = sb_in(s2, "in_blk", [P, TOPK * TILES, BW], fp16)
        rows = sb_in(s2, "rows", [P, BU, D], fp32)
        xT_hi = sb_in(s2, "xT_hi", [P, BU, KC, P], fp32r)
        xT_lo = sb_in(s2, "xT_lo", [P, BU, KC, P], fp32r)
        y_raw = sb_in(s2, "y_raw", [P, BU, D], fp32)
        y_sb = sb_in(s2, "y_sb", [P, BU, D], fp32)
        prod = sb_in(s2, "prod", [P, TILES, E], fp32)
        rank_of = sb_in(s2, "rank_of", [P, TOPK, TILES], fp32)
        first_of = sb_in(s2, "first_of", [P, TOPK, TILES], fp32)
        rank_i = sb_in(s2, "rank_i", [P, TOPK, TILES], i32)
        slot_i = sb_in(s2, "slot_i", [P, TOPK, TILES], i32)
        blk_i = sb_in(s2, "blk_i", [P, TOPK, TILES], i32)
        rank_blk = sb_in(s2, "rank_blk", [P, TOPK, TILES], fp32)
        count_i = sb_in(s2, "count_i", [P, E], i32)
        nblk_i = sb_in(s2, "nblk_i", [P, E], i32)
        nblk = sb_in(s2, "nblk", [P, E], fp32)
        blk_end = sb_in(s2, "blk_end", [P, E], fp32)
        blk_first = sb_in(s2, "blk_first", [P, E], fp32)
        past = sb_in(s2, "past", [1, BW, E], fp32)
        n_past = sb_in(s2, "n_past", [1, BW], fp32)
        pad_at = sb_in(s2, "pad_at", [P, BW], fp32)
        s2.close()

        tp = [ctx.enter_context(nc.psum_tensor(f"tp{i}", [P, D], fp32)) for i in range(2)]
        gb = [ctx.enter_context(nc.psum_tensor(f"gb{i}", [P, D], fp32)) for i in range(2)]
        sc = [ctx.enter_context(nc.psum_tensor(f"sc{i}", [P, D], fp32)) for i in range(2)]
        pvb = ctx.enter_context(nc.psum_tensor("pvb", [P, D], fp32))
        mb = ctx.enter_context(nc.psum_tensor("mb", [P, D], fp32))
        m_ps = [gb[0], gb[1], sc[0], sc[1]]
        w_ps, u_ps, bb_ps = mb[:, 0:KC], mb[:, KC:2 * KC], mb[:, 2 * KC:2 * KC + 1]
        r_ps = mb[:, 16:16 + 2 * TJ].rearrange("p (j c) -> p j c", c=2)
        l_ps = mb[:, 32:32 + TJ * E].rearrange("p (j e) -> p j e", e=E)
        rk_ps = mb[:, 64:64 + TJ * E].rearrange("p (j e) -> p j e", e=E)
        cnt_ps = mb[:, 96:96 + E]
        table_ps = pvb[:, 0:BW]
        tb = [tp[0], tp[1], mb]
        yb = [gb[0], gb[1], sc[0]]
        tpv = [t[:, :].rearrange("p (k t) -> p k t", k=KC) for t in tp]
        tbv = [t[:, :].rearrange("p (k t) -> p k t", k=KC) for t in tb]

        proj_in = sem("proj_in"); bias_in = sem("bias_in"); small_in = sem("small_in")
        x_first = [sem(f"x_first{g}") for g in range(3)]
        x_in = sem("x_in"); c_first = sem("c_first"); c_in = sem("c_in"); w_in = sem("w_in"); be_in = sem("be_in")
        x1_stored = sem("x1_stored"); h_stored = sem("h_stored"); pad_stored = sem("pad_stored")
        filled = sem("filled"); const_done = sem("const_done"); tanh_done = sem("tanh_done"); gain_done = sem("gain_done")
        bq_spread = sem("bq_spread")
        m_done = sem("m_done"); vec_done = sem("vec_done"); m_hi_done = sem("m_hi_done"); m_lo_done = sem("m_lo_done")
        vec_evac = sem("vec_evac"); u_hi_done = sem("u_hi_done")
        st1_step = sem("st1_step"); rstd1_done = sem("rstd1_done"); a_ready = sem("a_ready")
        aT_done = sem("aT_done"); aT_hi_done = sem("aT_hi_done"); aT_lo_done = sem("aT_lo_done")
        cT_done = sem("cT_done"); cT_evac = sem("cT_evac")
        g_done = sem("g_done"); g_evac = sem("g_evac")
        scores_done = sem("scores_done"); peak_done = sem("peak_done"); neg_done = sem("neg_done")
        exp_done = sem("exp_done"); inv_done = sem("inv_done"); att_gain_done = sem("att_gain_done")
        pt_done = sem("pt_done"); pt_evac = sem("pt_evac"); pv_done = sem("pv_done"); x1_ready = sem("x1_ready")
        st2_step = sem("st2_step"); rstd2_done = sem("rstd2_done"); h_ready = sem("h_ready")
        hT_done = sem("hT_done"); hT_evac = sem("hT_evac"); logits_done = sem("logits_done"); mask_step = sem("mask_step")
        mask_ready = sem("mask_ready"); misc_done = sem("misc_done"); row_summed = sem("row_summed")
        misc_read = sem("misc_read")
        w_hi_done = sem("w_hi_done"); w_lo_done = sem("w_lo_done")
        count_done = sem("count_done"); route_step = sem("route_step"); slot_hot = sem("slot_hot"); blk_hot = sem("blk_hot")
        table_done = sem("table_done"); rows_known = sem("rows_known"); expert_known = sem("expert_known")
        row_in = [sem(f"row_in{u}") for u in range(BU)]
        xT_done = sem("xT_done"); xT_hi_done = sem("xT_hi_done"); xT_lo_done = sem("xT_lo_done")
        y_done = sem("y_done"); y_biased = sem("y_biased"); y_ready = sem("y_ready"); added = sem("added")
        gather_known = sem("gather_known"); add_known = sem("add_known")

        block = ctx.enter_context(nc.Block())

        @block.sync
        def _(sp):
            sp.dma_start(wq_sb[:, :, :], Wq.rearrange("(p k) x -> p k x", p=P)).then_inc(proj_in, 16)
            sp.dma_start(wk_sb[:, :, :], Wk.rearrange("(p k) x -> p k x", p=P)).then_inc(proj_in, 16)
            sp.dma_start(x_sb[:, 0], x_v[:, 0]).then_inc(x_first[0], 16)
            sp.dma_start(bqk[:, 0, :], bq.rearrange("(p k) -> p k", p=P)).then_inc(bias_in, 16)
            sp.dma_start(bqk[:, 1, :], bk.rearrange("(p k) -> p k", p=P)).then_inc(bias_in, 16)
            sp.dma_start(x_sb[:, 1], x_v[:, 1]).then_inc(x_first[1], 16)
            sp.dma_start(c_sb[:, 0], c_v[:, 0]).then_inc(c_first, 16)
            sp.dma_start(gates[:, 0:1], g_x[None, :].to_broadcast([P, 1])).then_inc(small_in, 16)
            sp.dma_start(gates[:, 1:2], g_f[None, :].to_broadcast([P, 1])).then_inc(small_in, 16)
            sp.dma_start(bg_sb[:, :], bg[None, :].to_broadcast([P, E])).then_inc(small_in, 16)
            sp.dma_start(wg_sb[:, :, :], Wg.rearrange("(k p) e -> p k e", p=P)).then_inc(small_in, 16)
            sp.dma_start(x_sb[:, 2], x_v[:, 2]).then_inc(x_first[2], 16)
            sp.dma_start(c_sb[:, 1], c_v[:, 1]).then_inc(c_in, 16)
            sp.dma_start(x_sb[:, 3], x_v[:, 3]).then_inc(x_in, 16)

            def store(g, first):
                sp.wait_ge(x1_ready, TJ * g + TJ)
                sp.dma_start(out_v[:, ds(g, 1)], x_sb[:, ds(g % XR, 1)]).then_inc(x1_stored, 16)
                sp.wait_ge(h_ready, TJ * g + TJ)
                if not first:
                    sp.wait_ge(h_stored, 16 * g)
                sp.dma_start(h_v[:, ds(g, 1)], h_sb[:, None]).then_inc(h_stored, 16)
                sp.wait_ge(x1_stored, 16 * g + 16)

            def load_x(g):
                sp.wait_ge(x_in, 16 * g + 16)
                sp.dma_start(x_sb[:, ds(g % XR, 1)], x_v[:, ds(g + XR, 1)]).then_inc(x_in, 16)

            def load_c(g, parity):
                sp.wait_ge(pv_done, TJ * g + TJ)
                sp.wait_ge(c_in, 16 * g + 16)
                sp.dma_start(c_sb[:, parity:parity + 1], c_v[:, ds(g + 2, 1)]).then_inc(c_in, 16)

            sp.dma_start(out[N:N + P, :], x.rearrange("b s d -> (b s) d")[0:P, :]).then_inc(pad_stored, 16)

            store(0, True)
            sp.wait_ge(pad_stored, 16)
            load_c(0, 0)
            load_x(0)
            store(1, False)
            load_c(1, 1)
            load_x(1)
            with sp.Fori(1, GROUPS // 2 - 2) as i:
                for parity in range(2):
                    g = 2 * i + parity
                    store(g, False)
                    load_c(g, parity)
                    load_x(g)
            for g in range(GROUPS - XR, GROUPS):
                store(g, False)
                if g + 2 < GROUPS:
                    load_c(g, g % 2)
            sp.wait_ge(misc_read, GROUPS + 1)
            sp.wait_ge(h_stored, 16 * GROUPS)
            sp.wait_ge(w_lo_done, HALVES)
            sp.dma_start(be_sb[:, :, :], be[None, :, :].to_broadcast([P, E, D])).then_inc(be_in, 16)
            sp.wait_ge(added, 16 * BLOCKS)

        @block.scalar
        def _(act):
            act.wait_ge(small_in, 64)
            nc.scalar.activation(tanh_g[:, :], gates[:, :], ACT.Tanh).then_inc(tanh_done, 1)
            for c in range(KC):
                act.wait_ge(m_done, c + 1)
                nc.scalar.copy(m_hi[:, c], m_ps[c][:, :]).then_inc(m_hi_done, 1)

            def evac_a(g, j):
                act.wait_ge(aT_done, TJ * g + j + 1)
                nc.scalar.copy(aT_hi[:, :, j * P:(j + 1) * P], tpv[j]).then_inc(aT_hi_done, 1)

            def evac_g(g):
                for c in range(KC):
                    act.wait_ge(g_done, KC * g + c + 1)
                    nc.scalar.activation(gT[:, c], gb[c % 2][:, 0:GT], ACT.Identity,
                                         bias=w_vec[:, c:c + 1]).then_inc(g_evac, 1)

            for j in range(TJ):
                evac_a(0, j)
            act.wait_ge(vec_evac, 1)
            evac_g(0)
            act.wait_ge(const_done, 1)

            def group(g, first, last):
                for j in range(TJ):
                    act.wait_ge(cT_done, TJ * g + j + 1)
                    nc.scalar.copy(cT[:, j], tpv[j]).then_inc(cT_evac, 1)
                for j in range(TJ):
                    if not last:
                        evac_a(g + 1, j)
                    act.wait_ge(neg_done, TJ * g + j + 1)
                    for r0 in (0, S):
                        rr = slice(r0, r0 + S)
                        e = nc.scalar.activation(p_sb[rr, j, r0:r0 + S], s_sb[rr, j], ACT.Exp,
                                                 bias=neg_peak[rr, j:j + 1], scale=SCALE,
                                                 accum_out=exp_sum[rr, j:j + 1])
                    e.then_inc(exp_done, 1)
                if not first:
                    evac_h(g - 1)
                if not last:
                    evac_g(g + 1)

            def evac_h(g):
                for j in range(TJ):
                    act.wait_ge(hT_done, TJ * g + j + 1)
                    nc.scalar.copy(hT[:, j], tpv[j]).then_inc(hT_evac, 1)

            group(0, True, False)
            with act.Fori(1, GROUPS - 1) as g:
                group(g, False, False)
            group(GROUPS - 1, False, True)
            evac_h(GROUPS - 1)

            def block_hi(b, u):
                act.wait_ge(xT_done, b + 1)
                nc.scalar.copy(xT_hi[:, u], tbv[u]).then_inc(xT_hi_done, 1)

            act.wait_ge(misc_read, GROUPS + 1)
            with act.Fori(0, BLOCKS // BU) as i:
                for u in range(BU):
                    block_hi(i * BU + u, u)

        @block.vector
        def _(dve):
            nc.vector.memset(half_neg[:, :], -0.5).then_inc(filled, 1)
            nc.vector.memset(ident[:, :], 1.0).then_inc(filled, 1)
            nc.vector.memset(ones_b[:, :], 1.0).then_inc(filled, 1)
            nc.vector.memset(earlier[:, :], 1.0).then_inc(filled, 1)
            nc.vector.memset(p_sb[:, :, :], 0.0).then_inc(const_done, 1)
            nc.vector.memset(ones8[:, :], 1.0)
            nc.vector.memset(taken[:, :], 0.0).then_inc(mask_step, 1)

            def stats1(q, g):
                for j in range(TJ):
                    nc.vector.bn_stats(st1[:, j], x_sb[:, ds(g % XR, 1), j]).then_inc(st1_step, 1)
                dve.drain()
                for j in range(TJ):
                    nc.vector.bn_aggr(mv1[:, j], st1[:, j]).then_inc(st1_step, 1)
                dve.wait_ge(st1_step, 5 * q + 4)
                nc.vector.tensor_scalar(ve1[:, :], mv1[:, :, 1], EPS, None, ALU.add).then_inc(st1_step, 1)

            def norm1(q, g, first):
                dve.wait_ge(rstd1_done, q + 1)
                for j in range(TJ):
                    if not first:
                        dve.wait_ge(aT_done, TJ * (q - 1) + j + 1)
                    nc.vector.tensor_scalar(a_sb[:, j], x_sb[:, ds(g % XR, 1), j], mv1[:, j, 0:1],
                                            rstd1[:, j:j + 1], ALU.subtract, ALU.mult).then_inc(a_ready, 1)

            def lo_a(g, j):
                dve.wait_ge(aT_hi_done, TJ * g + j + 1)
                t = slice(j * P, (j + 1) * P)
                nc.vector.tensor_tensor(aT_lo[:, :, t], tpv[j], aT_hi[:, :, t].bitcast(fp32),
                                        ALU.subtract).then_inc(aT_lo_done, 1)

            def read_misc(g, ranks, rows_):
                dve.wait_ge(misc_done, g + 1)
                last = None
                if ranks:
                    last = nc.vector.tensor_copy(rank[:, ds(TJ * (g - 2), TJ), :], rk_ps)
                if rows_:
                    if last is not None:
                        last.then_inc(row_summed, 1)
                    nc.vector.tensor_reduce(row_sum[:, :], r_ps, AX.X, ALU.add).then_inc(misc_read, 1)
                    dve.wait_ge(misc_read, g + 1)
                    nc.vector.tensor_scalar(row_term[:, :], row_sum[:, :], bb[:, 0:1], None,
                                            ALU.add).then_inc(row_summed, 1)
                else:
                    last.then_inc(misc_read, 1)

            dve.wait_ge(x_first[0], 16)
            stats1(0, 0)
            norm1(0, 0, True)
            dve.wait_ge(bias_in, 32)
            nc.vector.tensor_copy(bq_rows[:, :, :], bqk[:, 0, :, None].to_broadcast([P, KC, P])).then_inc(bq_spread, 1)
            for c in range(KC):
                dve.wait_ge(m_hi_done, c + 1)
                nc.vector.tensor_tensor(m_lo[:, c], m_ps[c][:, :], m_hi[:, c].bitcast(fp32),
                                        ALU.subtract).then_inc(m_lo_done, 1)
            dve.wait_ge(vec_done, 1)
            nc.vector.tensor_copy(u_vec[:, :, 0:1], u_ps[:, :, None]).then_inc(u_hi_done, 1)
            nc.vector.tensor_copy(bb[:, :], bb_ps)
            nc.vector.tensor_copy(w_vec[:, :], w_ps)
            dve.wait_ge(u_hi_done, 1)
            nc.vector.tensor_tensor(u_vec[:, :, 1:2], u_ps[:, :, None], u_vec[:, :, 0:1].bitcast(fp32),
                                    ALU.subtract).then_inc(vec_evac, 1)
            for j in range(TJ):
                lo_a(0, j)
            dve.wait_ge(x_first[1], 16)
            stats1(1, 1)
            norm1(1, 1, False)
            dve.wait_ge(tanh_done, 1)
            nc.vector.tensor_scalar(ffn_gain[:, :], tanh_g[:, 1:2], 1.0 / TOPK, None, ALU.mult).then_inc(gain_done, 1)
            read_misc(0, False, True)

            def row_terms_in(g, first):
                return 1 if first else 2 * g

            def soft(g, j, first):
                dve.wait_ge(scores_done, TJ * g + j + 1)
                if j == 0:
                    dve.wait_ge(row_summed, 1 if first else 2 * g)
                for r0 in (0, S):
                    rr = slice(r0, r0 + S)
                    nc.vector.tensor_scalar(s_sb[rr, j], sc[j][rr, r0:r0 + S], row_term[rr, j:j + 1], None,
                                            ALU.add, ALU.max, accum_out=peak[rr, j:j + 1]).then_inc(peak_done, 1)
                dve.wait_ge(peak_done, 2 * (TJ * g + j + 1))
                nc.vector.tensor_scalar(neg_peak[:, j:j + 1], peak[:, j:j + 1], -SCALE, None,
                                        ALU.mult).then_inc(neg_done, 1)

            MS = 10

            def masks(g):
                b0 = MS * g + 1
                dve.wait_ge(logits_done, g + 1)
                nc.vector.tensor_tensor(logit[:, :, :], l_ps, bg_sb[:, None, :].to_broadcast([P, TJ, E]),
                                        ALU.add).then_inc(mask_step, 1)
                dve.drain()
                for j in range(TJ):
                    nc.vector.max(best[:, j], logit[:, j]).then_inc(mask_step, 1)
                dve.drain()
                for j in range(TJ):
                    nc.vector.max_index(best_at[:, j], best[:, j], logit[:, j]).then_inc(mask_step, 1)
                dve.wait_ge(mask_step, b0 + 5)
                nc.vector.tensor_copy(best_f[:, :, :], best_at[:, :, 0:TOPK]).then_inc(mask_step, 1)
                dve.wait_ge(mask_step, b0 + 6)
                for c in range(TOPK):
                    nc.vector.tensor_tensor(chosen[:, c, ds(TJ * g, TJ), :],
                                            iota_e[:, None, :].to_broadcast([P, TJ, E]),
                                            best_f[:, :, c:c + 1].to_broadcast([P, TJ, E]),
                                            ALU.is_equal).then_inc(mask_step, 1)
                dve.wait_ge(mask_step, b0 + 8)
                nc.vector.tensor_tensor(mask[:, :, :], chosen[:, 0, ds(TJ * g, TJ), :], chosen[:, 1, ds(TJ * g, TJ), :],
                                        ALU.add).then_inc(mask_ready, 1)

            def taken_more(g):
                b0 = MS * g + 1
                nc.vector.tensor_tensor(taken[:, :], taken[:, :], mask[:, 0], ALU.add).then_inc(mask_step, 1)
                dve.wait_ge(mask_step, b0 + 9)
                nc.vector.tensor_tensor(taken[:, :], taken[:, :], mask[:, 1], ALU.add).then_inc(mask_step, 1)

            def group(g, first, last, second_last):
                for j in range(TJ):
                    if not last:
                        lo_a(g + 1, j)
                    soft(g, j, first)
                ahead = not (last or second_last)
                if ahead:
                    if first:
                        dve.wait_ge(x_first[2], 16)
                    else:
                        dve.wait_ge(x_in, 16 * g)
                    stats1(g + 2, g + 2)
                if not first:
                    masks(g - 1)
                dve.wait_ge(exp_done, TJ * g + TJ)
                nc.vector.reciprocal(exp_inv[:, :], exp_sum[:, :]).then_inc(inv_done, 1)
                if ahead:
                    norm1(g + 2, g + 2, False)
                dve.wait_ge(inv_done, g + 1)
                nc.vector.tensor_scalar(att_gain[:, :], exp_inv[:, :], tanh_g[:, 0:1], None,
                                        ALU.mult).then_inc(att_gain_done, 1)
                if not (first and last):
                    read_misc(g + 1, not first, not last)
                if not first:
                    taken_more(g - 1)
                for j in range(TJ):
                    dve.wait_ge(pt_done, TJ * g + j + 1)
                    nc.vector.tensor_copy(pT_sb[:, j], sc[j][:, P:2 * P]).then_inc(pt_evac, 1)
                dve.wait_ge(att_gain_done, g + 1)
                xg = x_sb[:, ds(g % XR, 1)]
                for j in range(TJ):
                    dve.wait_ge(pv_done, TJ * g + j + 1)
                    nc.vector.scalar_tensor_tensor(x_sb[:, ds(g % XR, 1), j], pvb[:, :], att_gain[:, j:j + 1],
                                                   x_sb[:, ds(g % XR, 1), j], ALU.mult, ALU.add).then_inc(x1_ready, 1)
                dve.drain()
                for j in range(TJ):
                    nc.vector.bn_stats(st2[:, j], x_sb[:, ds(g % XR, 1), j]).then_inc(st2_step, 1)
                dve.drain()
                for j in range(TJ):
                    nc.vector.bn_aggr(mv2[:, j], st2[:, j]).then_inc(st2_step, 1)
                dve.wait_ge(st2_step, 5 * g + 4)
                nc.vector.tensor_scalar(ve2[:, :], mv2[:, :, 1], EPS, None, ALU.add).then_inc(st2_step, 1)
                dve.wait_ge(rstd2_done, g + 1)
                if not first:
                    dve.wait_ge(hT_done, TJ * g)
                    dve.wait_ge(h_stored, 16 * g)
                for j in range(TJ):
                    nc.vector.tensor_scalar(h_sb[:, j], x_sb[:, ds(g % XR, 1), j], mv2[:, j, 0:1],
                                            rstd2[:, j:j + 1], ALU.subtract, ALU.mult).then_inc(h_ready, 1)

            group(0, True, False, False)
            with dve.Fori(1, GROUPS - 2) as g:
                group(g, False, False, False)
            group(GROUPS - 2, False, False, True)
            group(GROUPS - 1, False, True, False)
            masks(GROUPS - 1)
            read_misc(GROUPS + 1, True, False)
            taken_more(GROUPS - 1)

            dve.wait_ge(misc_read, GROUPS + 2)
            step = 0

            def after(n):
                dve.wait_ge(route_step, n)

            dve.wait_ge(h_stored, 16 * GROUPS)
            dve.wait_ge(w_lo_done, HALVES)
            for c in range(TOPK):
                if c:
                    after(2)
                nc.vector.tensor_tensor(prod[:, :, :], rank[:, :, :], chosen[:, c], ALU.mult).then_inc(route_step, 1)
                after(2 * c + 1)
                nc.vector.tensor_reduce(rank_of[:, c], prod[:, :, :], AX.X, ALU.add).then_inc(route_step, 1)
            after(4)
            nc.vector.tensor_copy(rank_i[:, :, :], rank_of[:, :, :]).then_inc(route_step, 1)
            after(5)
            nc.vector.tensor_scalar(slot_i[:, :, :], rank_i[:, :, :], P - 1, None,
                                    ALU.bitwise_and).then_inc(route_step, 1)
            nc.vector.tensor_scalar(blk_i[:, :, :], rank_i[:, :, :], P.bit_length() - 1, None,
                                    ALU.arith_shift_right).then_inc(route_step, 1)
            after(7)
            nc.vector.tensor_copy(slot_of[:, :, :], slot_i[:, :, :]).then_inc(route_step, 1)
            nc.vector.tensor_copy(rank_blk[:, :, :], blk_i[:, :, :]).then_inc(route_step, 1)
            dve.wait_ge(count_done, 1)
            nc.vector.tensor_scalar(count_i[:, :], cnt_ps, float(P - 1), None, ALU.add).then_inc(route_step, 1)
            after(10)
            nc.vector.tensor_scalar(nblk_i[:, :], count_i[:, :], P.bit_length() - 1, None,
                                    ALU.arith_shift_right).then_inc(route_step, 1)
            after(11)
            nc.vector.tensor_copy(nblk[:, :], nblk_i[:, :]).then_inc(route_step, 1)
            after(12)
            nc.vector.tensor_tensor_scan(blk_end[:, :], ones8[:, :], nblk[:, :], 0.0, ALU.mult,
                                         ALU.add).then_inc(route_step, 1)
            after(13)
            nc.vector.tensor_tensor(blk_first[:, :], blk_end[:, :], nblk[:, :], ALU.subtract).then_inc(route_step, 1)
            for c in range(TOPK):
                after(14 + 2 * c)
                nc.vector.tensor_tensor(prod[:, :, :], chosen[:, c], blk_first[:, None, :].to_broadcast([P, TILES, E]),
                                        ALU.mult).then_inc(route_step, 1)
                after(15 + 2 * c)
                nc.vector.tensor_reduce(first_of[:, c], prod[:, :, :], AX.X, ALU.add).then_inc(route_step, 1)
            after(18)
            nc.vector.tensor_tensor(blk_of[:, :, :], rank_blk[:, :, :], first_of[:, :, :],
                                    ALU.add).then_inc(route_step, 1)
            after(19)
            for c in range(TOPK):
                for t in range(TILES):
                    n = c * TILES + t
                    nc.vector.tensor_scalar(in_slot[:, n], iota_p[:, :], slot_of[:, c, t:t + 1], None,
                                            ALU.is_equal).then_inc(slot_hot, 1)
                    nc.vector.tensor_scalar(in_blk[:, n], iota_blk[:, :], blk_of[:, c, t:t + 1],
                                            token1[:, t:t + 1], ALU.is_equal, ALU.mult).then_inc(blk_hot, 1)
            nc.vector.tensor_tensor(past[:, :, :], iota_blk[0:1, :, None].to_broadcast([1, BW, E]),
                                    blk_end[0:1, None, :].to_broadcast([1, BW, E]), ALU.is_ge).then_inc(route_step, 1)
            after(20)
            nc.vector.tensor_reduce(n_past[:, :], past[:, :, :], AX.X, ALU.add).then_inc(route_step, 1)
            after(21)
            nc.vector.tensor_scalar(expert_of[:, :], n_past[:, :], float(E - 1), None,
                                    ALU.min).then_inc(expert_known, 1)
            dve.wait_ge(table_done, 1)
            nc.vector.tensor_scalar(gather_row[:, :], table_ps, -1.0, 0.0, ALU.add, ALU.max).then_inc(rows_known, 1)
            nc.vector.tensor_scalar(pad_at[:, :], table_ps, 0.0, pad_row[:, 0:1], ALU.is_equal,
                                    ALU.mult).then_inc(route_step, 1)
            after(22)
            nc.vector.scalar_tensor_tensor(add_row[:, :], table_ps, -1.0, pad_at[:, :], ALU.add,
                                           ALU.add).then_inc(rows_known, 1)

            dve.wait_ge(be_in, 16)
            dve.wait_ge(gain_done, 1)
            dve.wait_ge(expert_known, 1)

            def block_lo(b, u):
                dve.wait_ge(xT_hi_done, b + 1)
                nc.vector.tensor_tensor(xT_lo[:, u], tbv[u], xT_hi[:, u].bitcast(fp32),
                                        ALU.subtract).then_inc(xT_lo_done, 1)

            def block_y(b, u, first):
                e = dve.value_load(expert_of[0:1, ds(b, 1)], min_val=0, max_val=E - 1)
                dve.wait_ge(y_done, b + 1)
                nc.vector.tensor_tensor(y_raw[:, u], yb[u][:, :], be_sb[:, ds(e, 1), :], ALU.add).then_inc(y_biased, 1)
                if not first:
                    dve.wait_ge(added, 16 * (b - BU + 1))
                dve.wait_ge(y_biased, b + 1)
                nc.vector.tensor_scalar(y_sb[:, u], y_raw[:, u], 0.0, ffn_gain[:, 0:1], ALU.max,
                                        ALU.mult).then_inc(y_ready, 1)

            block_lo(0, 0)
            for u in range(BU):
                block_lo(u + 1, (u + 1) % BU)
                block_y(u, u, True)
            with dve.Fori(1, BLOCKS // BU - 1) as i:
                for u in range(BU):
                    block_lo(i * BU + u + 1, (u + 1) % BU)
                    block_y(i * BU + u, u, False)
            for u in range(BU):
                b = BLOCKS - BU + u
                if u < BU - 1:
                    block_lo(b + 1, (u + 1) % BU)
                block_y(b, u, False)

        @block.gpsimd
        def _(pool):
            def load_w(n):
                pool.dma_start(w_raw[:, :, :], we_v[:, ds(HK * n, HK), :]).then_inc(w_in, 16)

            def split_w(n, more):
                pool.wait_ge(w_in, 16 * n + 16)
                nc.gpsimd.tensor_copy(we_hi[:, ds(HK * n, HK), :], w_raw[:, :, :]).then_inc(w_hi_done, 1)
                pool.wait_ge(w_hi_done, n + 1)
                nc.gpsimd.tensor_tensor(we_lo[:, ds(HK * n, HK), :], w_raw[:, :, :],
                                        we_hi[:, ds(HK * n, HK), :].bitcast(fp32), ALU.subtract).then_inc(w_lo_done, 1)
                if more:
                    pool.wait_ge(w_lo_done, n + 1)
                    load_w(n + 1)

            def rstd(q, steps, var_eps, rstd_, done):
                pool.wait_ge(steps, 5 * q + 5)
                nc.gpsimd.tensor_tensor(rstd_[:, :], var_eps[:, :], half_neg[:, :], ALU.pow).then_inc(done, 1)

            nc.gpsimd.memset(gate[:, :], 0.0)
            pool.wait_ge(filled, 4)
            nc.gpsimd.affine_select(ident[:, :], ident[:, :], [[1, P]], ALU.is_equal, 0.0, base=0,
                                    channel_multiplier=-1).then_inc(const_done, 1)
            nc.gpsimd.affine_select(earlier[:, :], earlier[:, :], [[1, P]], ALU.is_gt, 0.0, base=0,
                                    channel_multiplier=-1).then_inc(const_done, 1)
            rstd(0, st1_step, ve1, rstd1, rstd1_done)
            nc.gpsimd.iota(iota_e[:, :], [[1, E]], base=0, channel_multiplier=0,
                           allow_small_or_imprecise_dtypes=True).then_inc(const_done, 1)
            nc.gpsimd.iota(iota_p[:, :], [[1, P]], base=0, channel_multiplier=0,
                           allow_small_or_imprecise_dtypes=True).then_inc(const_done, 1)
            nc.gpsimd.iota(iota_blk[:, :], [[1, BW]], base=0, channel_multiplier=0,
                           allow_small_or_imprecise_dtypes=True).then_inc(const_done, 1)
            nc.gpsimd.iota(token1[:, :], [[P, TILES]], base=1, channel_multiplier=1,
                           allow_small_or_imprecise_dtypes=True).then_inc(const_done, 1)
            nc.gpsimd.iota(pad_row[:, :], [[1, 1]], base=N + 1, channel_multiplier=1,
                           allow_small_or_imprecise_dtypes=True).then_inc(const_done, 1)
            load_w(0)
            rstd(1, st1_step, ve1, rstd1, rstd1_done)

            def group(g, ahead, more):
                if ahead:
                    rstd(g + 2, st1_step, ve1, rstd1, rstd1_done)
                split_w(2 * g, True)
                split_w(2 * g + 1, more)
                rstd(g, st2_step, ve2, rstd2, rstd2_done)

            with pool.Fori(0, GROUPS - 2) as g:
                group(g, True, True)
            group(GROUPS - 2, False, True)
            group(GROUPS - 1, False, False)

            def gather(b, u):
                pool.indirect_dma_start(out=rows[:, u, :], out_offset=None, in_=h_dram,
                                        in_offset=bass.IndirectOffsetOnAxis(ap=gather_at[:, u:u + 1], axis=0)
                                        ).then_inc(row_in[u], 16)

            def add(b, u):
                pool.indirect_dma_start(out=out, out_offset=bass.IndirectOffsetOnAxis(ap=add_at[:, u:u + 1], axis=0),
                                        in_=y_sb[:, u, :], in_offset=None, compute_op=ALU.add).then_inc(added, 16)

            pool.wait_ge(rows_known, 1)
            for u in range(BU):
                nc.gpsimd.tensor_copy(gather_at[:, u:u + 1], gather_row[:, u:u + 1]).then_inc(gather_known, 1)
            pool.wait_ge(gather_known, BU)
            pool.wait_ge(h_stored, 16 * GROUPS)
            for u in range(BU):
                gather(u, u)
            pool.wait_ge(rows_known, 2)
            pool.wait_ge(x1_stored, 16 * GROUPS)
            pool.wait_ge(pad_stored, 16)

            def turn(b, u, first, more):
                nc.gpsimd.tensor_copy(add_at[:, u:u + 1], add_row[:, ds(b, 1)]).then_inc(add_known, 1)
                if more:
                    pool.wait_ge(xT_done, b + 1)
                    nc.gpsimd.tensor_copy(gather_at[:, u:u + 1], gather_row[:, ds(b + BU, 1)]).then_inc(gather_known, 1)
                    pool.wait_ge(gather_known, b + BU + 1)
                pool.wait_ge(add_known, b + 1)
                pool.wait_ge(y_ready, b + 1)
                if not first:
                    pool.wait_ge(added, 16 * b)
                nc.gpsimd.tensor_tensor(gate[:, :], gate[:, :], gate[:, :], ALU.add)
                add(b, u)
                if more:
                    gather(b + BU, u)

            for u in range(BU):
                turn(u, u, u == 0, True)
            with pool.Fori(1, BLOCKS // BU - 1) as i:
                for u in range(BU):
                    turn(i * BU + u, u, False, True)
            for u in range(BU):
                turn(BLOCKS - BU + u, u, False, False)
            pool.wait_ge(added, 16 * BLOCKS)

        @block.tensor
        def _(pe):
            def chunks4(dst, src, done, lane):
                for k in range(KC):
                    t = nc.tensor.transpose(dst[:, k * P:(k + 1) * P], src(k), ident[:, :])
                t.then_inc(done, 1)

            def product3(dst, k3, k_hi, k_lo, rhs_hi, rhs_lo):
                for k in range(k3):
                    nc.tensor.matmul(dst, k_hi(k), rhs_hi(k), start=(k == 0), stop=False)
                    nc.tensor.matmul(dst, k_hi(k), rhs_lo(k), start=False, stop=False)
                    last = nc.tensor.matmul(dst, k_lo(k), rhs_hi(k), start=False, stop=(k == k3 - 1))
                return last

            pe.wait_ge(proj_in, 32)
            for c in range(KC):
                for k in range(KC):
                    m = nc.tensor.matmul(m_ps[c][:, :], wq_sb[:, k, c * P:(c + 1) * P], wk_sb[:, k, :],
                                         start=(k == 0), stop=(k == KC - 1))
                m.then_inc(m_done, 1)
            pe.wait_ge(bias_in, 32)
            for dst, w, b in ((w_ps, wk_sb, 0), (u_ps, wq_sb, 1)):
                for c in range(KC):
                    for k in range(KC):
                        nc.tensor.matmul(dst[:, c:c + 1], w[:, k, c * P:(c + 1) * P], bqk[:, b, k:k + 1],
                                         start=(k == 0), stop=(k == KC - 1))
            pe.wait_ge(bq_spread, 1)
            for k in range(KC):
                m = nc.tensor.matmul(bb_ps, bq_rows[:, k, :], bqk[:, 1, k:k + 1], start=(k == 0), stop=(k == KC - 1))
            m.then_inc(vec_done, 1)

            def transpose_a(g, j):
                pe.wait_ge(a_ready, TJ * g + j + 1)
                chunks4(tp[j], lambda k: a_sb[:, j, k * P:(k + 1) * P], aT_done, j)

            def product_g(g, c, first):
                if not first or c >= 2:
                    pe.wait_ge(g_evac, KC * g + c - 1)
                cc = slice(c * P, (c + 1) * P)
                product3(gb[c % 2][:, 0:GT], KC, lambda k: m_hi[:, k, cc], lambda k: m_lo[:, k, cc],
                         lambda k: aT_hi[:, k, :], lambda k: aT_lo[:, k, :]).then_inc(g_done, 1)

            def row_terms(first):
                for j in range(TJ):
                    t = slice(j * P, (j + 1) * P)
                    for k in range(KC):
                        nc.tensor.matmul(r_ps[:, j], aT_hi[:, k, t], u_vec[:, k, :], start=(k == 0), stop=False)
                        m = nc.tensor.matmul(r_ps[:, j], aT_lo[:, k, t], u_vec[:, k, :], start=False, stop=(k == KC - 1))
                return m

            pe.wait_ge(const_done, 2)
            for j in range(TJ):
                transpose_a(0, j)
            pe.wait_ge(m_lo_done, KC)
            pe.wait_ge(aT_lo_done, TJ)
            for c in range(KC):
                product_g(0, c, True)
            pe.wait_ge(vec_evac, 1)
            row_terms(True).then_inc(misc_done, 1)

            def transpose_h(g, waits):
                for j in range(TJ):
                    pe.wait_ge(h_ready, TJ * g + j + 1)
                    waits(j)
                    chunks4(tp[j], lambda k: h_sb[:, j, k * P:(k + 1) * P], hT_done, j)

            def logits(g):
                pe.wait_ge(hT_evac, TJ * g + TJ)
                pe.wait_ge(misc_read, g + 2)
                for j in range(TJ):
                    for k in range(KC):
                        m = nc.tensor.matmul(l_ps[:, j], hT[:, j, k, :], wg_sb[:, k, :], start=(k == 0), stop=(k == KC - 1))
                m.then_inc(logits_done, 1)

            def ranks(g):
                pe.wait_ge(mask_ready, g + 1)
                nc.tensor.matmul(rk_ps[:, 0], earlier[:, :], mask[:, 0], start=True, stop=False)
                m = nc.tensor.matmul(rk_ps[:, 0], ones_b[:, :], taken[:, :], start=False, stop=True)
                nc.tensor.matmul(rk_ps[:, 1], earlier[:, :], mask[:, 1], start=True, stop=False)
                nc.tensor.matmul(rk_ps[:, 1], ones_b[:, :], mask[:, 0], start=False, stop=False)
                return nc.tensor.matmul(rk_ps[:, 1], ones_b[:, :], taken[:, :], start=False, stop=True)

            def group(g, parity, first, last):
                if first:
                    pe.wait_ge(c_first, 16)
                else:
                    pe.wait_ge(c_in, 16 * g)
                for j in range(TJ):
                    chunks4(tp[j], lambda k: c_sb[:, parity, j, k * P:(k + 1) * P], cT_done, j)
                for j in range(TJ):
                    pe.wait_ge(cT_evac, TJ * g + j + 1)
                    if not last:
                        transpose_a(g + 1, j)
                    pe.wait_ge(g_evac, KC * g + KC)
                    if not first:
                        pe.wait_ge(pt_evac, TJ * (g - 1) + j + 1)
                    for k in range(KC):
                        m = nc.tensor.matmul(sc[j][:, 0:P], gT[:, k, j * P:(j + 1) * P], cT[:, j, k, :],
                                             start=(k == 0), stop=(k == KC - 1))
                    m.then_inc(scores_done, 1)
                if not first:
                    if last:
                        transpose_h(g - 1, lambda j: None)
                    else:
                        transpose_h(g - 1, lambda j: pe.wait_ge(aT_lo_done, TJ * (g + 1) + j + 1))
                if not last:
                    pe.wait_ge(aT_lo_done, TJ * (g + 1) + TJ)
                    product_g(g + 1, 0, False)
                    product_g(g + 1, 1, False)
                if not first:
                    logits(g - 1)
                if not last:
                    product_g(g + 1, 2, False)
                    product_g(g + 1, 3, False)
                done = None
                if not first:
                    done = ranks(g - 1)
                if not last:
                    if first:
                        pe.wait_ge(misc_read, 1)
                    done = row_terms(False)
                done.then_inc(misc_done, 1)
                for j in range(TJ):
                    pe.wait_ge(exp_done, TJ * g + j + 1)
                    nc.tensor.transpose(sc[j][:, P:2 * P], p_sb[:, j], ident[:, :]).then_inc(pt_done, 1)
                for j in range(TJ):
                    pe.wait_ge(pt_evac, TJ * g + j + 1)
                    if j or not first:
                        pe.wait_ge(x1_ready, TJ * g + j)
                    nc.tensor.matmul(pvb[:, :], pT_sb[:, j], c_sb[:, parity, j, :], start=True, stop=True).then_inc(pv_done, 1)

            pe.wait_ge(small_in, 64)
            group(0, 0, True, False)
            with pe.Fori(0, GROUPS // 2 - 1) as i:
                for parity in (1, 0):
                    group(2 * i + (2 - parity), parity, False, False)
            group(GROUPS - 1, 1, False, True)
            transpose_h(GROUPS - 1, lambda j: None)
            logits(GROUPS - 1)
            ranks(GROUPS - 1).then_inc(misc_done, 1)
            pe.wait_ge(misc_read, GROUPS + 2)
            pe.wait_ge(mask_step, 10 * GROUPS + 1)
            nc.tensor.matmul(cnt_ps, ones_b[:, :], taken[:, :], start=True, stop=True).then_inc(count_done, 1)
            for n in range(TOPK * TILES):
                pe.wait_ge(slot_hot, n + 1)
                pe.wait_ge(blk_hot, n + 1)
                m = nc.tensor.matmul(table_ps, in_slot[:, n], in_blk[:, n], start=(n == 0), stop=(n == TOPK * TILES - 1))
            m.then_inc(table_done, 1)

            def transpose_rows(b, u, first):
                pe.wait_ge(row_in[u], 16 * (b // BU) + 16 if isinstance(b, int) else first)
                chunks4(tb[u], lambda k: rows[:, u, k * P:(k + 1) * P], xT_done, u)

            def block_product(b, u, first):
                e = pe.value_load(expert_of[0:1, ds(b, 1)], min_val=0, max_val=E - 1)
                pe.wait_ge(xT_lo_done, b + 1)
                if not first:
                    pe.wait_ge(y_biased, b - BU + 1)
                product3(yb[u][:, :], KC, lambda k: xT_hi[:, u, k, :], lambda k: xT_lo[:, u, k, :],
                         lambda k: we_hi[:, ds(e * KC + k, 1), :], lambda k: we_lo[:, ds(e * KC + k, 1), :]).then_inc(y_done, 1)

            pe.wait_ge(expert_known, 1)
            transpose_rows(0, 0, None)
            for u in range(BU):
                transpose_rows(u + 1, (u + 1) % BU, None)
                block_product(u, u, True)
            with pe.Fori(1, BLOCKS // BU - 1) as i:
                for u in range(BU):
                    turn = 16 * i + 16 + (16 if u == BU - 1 else 0)
                    transpose_rows(i * BU + u + 1, (u + 1) % BU, turn)
                    block_product(i * BU + u, u, False)
            for u in range(BU):
                b = BLOCKS - BU + u
                if u < BU - 1:
                    transpose_rows(b + 1, (u + 1) % BU, None)
                block_product(b, u, False)


_INS = ["x", "ctx_4096", "g_xattn", "g_ffn", "L0_xattn_Wq", "L0_xattn_bq", "L0_xattn_Wk", "L0_xattn_bk",
        "L0_ffn_W_gate", "L0_ffn_b_gate", "L0_ffn_W_e", "L0_ffn_b_e"]


def kernel(**inputs):
    import numpy as _np
    import concourse.bacc as _bacc
    from concourse import mybir as _mybir
    from concourse.bass_utils import run_bass_kernel_spmd as _run

    nc = _bacc.Bacc("TRN2", target_bir_lowering=False, num_devices=1)
    arrays, args = {}, []
    for name in _INS:
        a = _np.ascontiguousarray(inputs[name])
        arrays[f"in_{name}"] = a
        args.append(nc.dram_tensor(f"in_{name}", a.shape, _mybir.dt.from_np(a.dtype), kind="ExternalInput").ap())
    out = nc.dram_tensor("out_rows", (N + P, D), _mybir.dt.float32, kind="ExternalOutput").ap()
    gated_xattn_moe(nc, *args, out)
    r = _run(nc, [arrays], core_ids=[0])
    return _np.asarray(r.results[0]["out_rows"])[:N].reshape(B, S, D)
```

```python
import concourse.bass as bass
from concourse import mybir
from contextlib import ExitStack

fp32 = mybir.dt.float32
fp32r = mybir.dt.float32r
fp16 = mybir.dt.float16
bf16 = mybir.dt.bfloat16
i32 = mybir.dt.int32
u32 = mybir.dt.uint32
ALU = mybir.AluOpType
ACT = mybir.ActivationFunctionType
AX = mybir.AxisListType
ds = bass.ds

P = 128
B, S, D = 32, 64, 512
E, TOPK = 8, 2
KC = D // P
N = B * S
TJ = 2
GT = TJ * P
GROUPS = N // GT
TILES = N // P
XR = 4
BLOCKS = (TOPK * N - E) // P + E
BU = 4
TURNS = (BLOCKS - 1) // BU
BW = BLOCKS + BLOCKS % 2
SCALE = float(D) ** -0.5
EPS = 1e-5
assert GROUPS % 2 == 0 and BLOCKS > TURNS * BU
assert GROUPS == E


def gated_xattn_moe(nc, x, ctx_, g_x, g_f, Wq, bq, Wk, bk, Wg, bg, We, be, out):
    x_v = x.rearrange("b s d -> (b s) d").rearrange("(g j p) d -> p g j d", j=TJ, p=P)
    c_v = ctx_.rearrange("b s d -> (b s) d").rearrange("(g j p) d -> p g j d", j=TJ, p=P)
    out_v = out[0:N, :].rearrange("(g j p) d -> p g j d", j=TJ, p=P)
    we_v = We.rearrange("e (k p) h -> p (e k) h", p=P)
    h_dram = nc.dram_tensor("h_dram", [N, D], fp32, kind="Internal").ap()
    h_v = h_dram.rearrange("(g j p) d -> p g j d", j=TJ, p=P)

    ctx = ExitStack()
    with ctx:
        def sb_in(stack, name, shape, dt):
            return stack.enter_context(nc.sbuf_tensor(name, shape, dt))

        def sem(name):
            return ctx.enter_context(nc.semaphore(name))

        def sb(name, shape, dt):
            return sb_in(ctx, name, shape, dt)

        we_hi = sb("we_hi", [P, E * KC, D], fp32r)
        loading = ExitStack()
        we_raw = sb_in(loading, "we_raw", [P, E * KC, D], fp32)
        loading.close()
        we_lo = sb("we_lo", [P, E * KC, D], fp32r)
        ident = sb("ident", [P, P], fp32)
        earlier = sb("earlier", [P, P], bf16)
        ones_b = sb("ones_b", [P, P], bf16)
        ones8 = sb("ones8", [P, E], fp32)
        iota_e = sb("iota_e", [P, E], fp32)
        iota_p = sb("iota_p", [P, P], fp16)
        iota_blk = sb("iota_blk", [P, BW], fp32)
        token1 = sb("token1", [P, TILES], fp32)
        pad_row = sb("pad_row", [P, 1], fp32)
        half_neg = sb("half_neg", [P, TJ], fp32)
        gates = sb("gates", [P, 2], fp32)
        tanh_g = sb("tanh_g", [P, 2], fp32)
        ffn_gain = sb("ffn_gain", [P, 1], fp32)
        chosen = sb("chosen", [P, TOPK, TILES, E], bf16)
        rank = sb("rank", [P, TILES, E], fp32)
        taken = sb("taken", [P, E], bf16)
        gather_row = sb("gather_row", [P, BW], u32)
        add_row = sb("add_row", [P, BW], u32)
        gather_at = sb("gather_at", [P, BU], u32)
        gate = sb("gate", [1, 1], fp32)
        add_at = sb("add_at", [P, BU], u32)
        expert_of = sb("expert_of", [1, BW], i32)

        s1 = ExitStack()
        x_sb = sb_in(s1, "x_sb", [P, XR, TJ, D], fp32)
        s0 = ExitStack()
        wq_sb = sb_in(s0, "wq_sb", [P, KC, D], fp32)
        wk_sb = sb_in(s0, "wk_sb", [P, KC, D], fp32)
        bqk = sb_in(s0, "bqk", [P, 2, KC], fp32)
        bk_rows = sb_in(s0, "bk_rows", [P, KC, P], fp32)
        s0.close()
        aT_hi = sb_in(s1, "aT_hi", [P, KC, GT], fp32r)
        aT_lo = sb_in(s1, "aT_lo", [P, KC, GT], fp32r)
        gT = sb_in(s1, "gT", [P, KC, GT], fp32)
        cT = sb_in(s1, "cT", [P, TJ, KC, P], fp32)
        hT = sb_in(s1, "hT", [P, TJ, KC, P], fp32)
        c_sb = sb_in(s1, "c_sb", [P, 2, TJ, D], fp32)
        m_hi = sb_in(s1, "m_hi", [P, KC, D], fp32r)
        m_lo = sb_in(s1, "m_lo", [P, KC, D], fp32r)
        a_sb = sb_in(s1, "a_sb", [P, TJ, D], fp32)
        h_sb = sb_in(s1, "h_sb", [P, TJ, D], fp32)
        wg_sb = sb_in(s1, "wg_sb", [P, KC, E], fp32)
        bg_sb = sb_in(s1, "bg_sb", [P, E], fp32)
        w_vec = sb_in(s1, "w_vec", [P, KC], fp32)
        u_rows = sb_in(s1, "u_rows", [P, D], fp32)
        bb = sb_in(s1, "bb", [P, 1], fp32)
        s_sb = sb_in(s1, "s_sb", [P, TJ, S], fp32)
        p_sb = sb_in(s1, "p_sb", [P, TJ, P], fp32)
        row_sum = sb_in(s1, "row_sum", [P, TJ], fp32)
        row_term = sb_in(s1, "row_term", [P, TJ], fp32)
        peak = sb_in(s1, "peak", [P, TJ], fp32)
        neg_peak = sb_in(s1, "neg_peak", [P, TJ], fp32)
        exp_sum = sb_in(s1, "exp_sum", [P, TJ], fp32)
        exp_inv = sb_in(s1, "exp_inv", [P, TJ], fp32)
        att_gain = sb_in(s1, "att_gain", [P, TJ], fp32)
        st1 = sb_in(s1, "st1", [P, TJ, 6], fp32)
        mv1 = sb_in(s1, "mv1", [P, TJ, 2], fp32)
        ve1 = sb_in(s1, "ve1", [P, TJ], fp32)
        rstd1 = sb_in(s1, "rstd1", [P, TJ], fp32)
        st2 = sb_in(s1, "st2", [P, TJ, 6], fp32)
        mv2 = sb_in(s1, "mv2", [P, TJ, 2], fp32)
        ve2 = sb_in(s1, "ve2", [P, TJ], fp32)
        rstd2 = sb_in(s1, "rstd2", [P, TJ], fp32)
        logit = sb_in(s1, "logit", [P, TJ, E], fp32)
        best = sb_in(s1, "best", [P, TJ, E], fp32)
        best_at = sb_in(s1, "best_at", [P, TJ, E], u32)
        best_f = sb_in(s1, "best_f", [P, TJ, TOPK], fp32)
        mask = sb_in(s1, "mask", [P, TJ, E], bf16)
        s1.close()
        s2 = ExitStack()
        be_sb = sb_in(s2, "be_sb", [P, E, D], fp32)
        in_slot = sb_in(s2, "in_slot", [P, TOPK * TILES, P], fp16)
        in_blk = sb_in(s2, "in_blk", [P, TOPK * TILES, BW], fp16)
        prod = sb_in(s2, "prod", [P, TILES, E], fp32)
        rank_of = sb_in(s2, "rank_of", [P, TOPK, TILES], fp32)
        first_of = sb_in(s2, "first_of", [P, TOPK, TILES], fp32)
        rank_i = sb_in(s2, "rank_i", [P, TOPK, TILES], i32)
        slot_i = sb_in(s2, "slot_i", [P, TOPK, TILES], i32)
        blk_i = sb_in(s2, "blk_i", [P, TOPK, TILES], i32)
        rank_blk = sb_in(s2, "rank_blk", [P, TOPK, TILES], fp32)
        count_i = sb_in(s2, "count_i", [P, E], i32)
        nblk_i = sb_in(s2, "nblk_i", [P, E], i32)
        nblk = sb_in(s2, "nblk", [P, E], fp32)
        blk_end = sb_in(s2, "blk_end", [P, E], fp32)
        blk_first = sb_in(s2, "blk_first", [P, E], fp32)
        past = sb_in(s2, "past", [1, BW, E], fp32)
        n_past = sb_in(s2, "n_past", [1, BW], fp32)
        pad_at = sb_in(s2, "pad_at", [P, BW], fp32)
        slot_of = sb_in(s2, "slot_of", [P, TOPK, TILES], fp32)
        blk_of = sb_in(s2, "blk_of", [P, TOPK, TILES], fp32)
        rows = sb_in(s2, "rows", [P, BU, D], fp32)
        xT_hi = sb_in(s2, "xT_hi", [P, BU, KC, P], fp32r)
        xT_lo = sb_in(s2, "xT_lo", [P, BU, KC, P], fp32r)
        y_raw = sb_in(s2, "y_raw", [P, BU, D], fp32)
        y_sb = sb_in(s2, "y_sb", [P, BU, D], fp32)
        s2.close()

        tp = [ctx.enter_context(nc.psum_tensor(f"tp{i}", [P, D], fp32)) for i in range(3)]
        gb = [ctx.enter_context(nc.psum_tensor(f"gb{i}", [P, D], fp32)) for i in range(2)]
        sc = [ctx.enter_context(nc.psum_tensor(f"sc{i}", [P, D], fp32)) for i in range(2)]
        mb = ctx.enter_context(nc.psum_tensor("mb", [P, D], fp32))
        m_ps = [gb[0], gb[1], sc[0], sc[1]]
        w_ps, bb_ps, u_ps = mb[:, 0:KC], mb[:, KC:KC + 1], tp[2]
        l_ps = mb[:, 32:32 + TJ * E].rearrange("p (j e) -> p j e", e=E)
        rk_ps = mb[:, 64:64 + TJ * E].rearrange("p (j e) -> p j e", e=E)
        cnt_ps = mb[:, 96:96 + E]
        table_ps = sc[0][:, 0:BW]
        tb = [tp[0], tp[1], tp[2], mb]
        yb = [gb[0], gb[1], sc[0], sc[1]]
        c_tp, a_tp, h_tp = (0, 1), (0, 2), (1, 2)
        tpv = [t[:, :].rearrange("p (k t) -> p k t", k=KC) for t in tp]
        tbv = [t[:, :].rearrange("p (k t) -> p k t", k=KC) for t in tb]

        proj_in = sem("proj_in"); bias_in = sem("bias_in"); small_in = sem("small_in")
        x_first = [sem(f"x_first{g}") for g in range(3)]
        x_in = sem("x_in"); c_first = sem("c_first"); c_in = sem("c_in"); w_in = sem("w_in"); be_in = sem("be_in")
        x1_stored = sem("x1_stored"); h_stored = sem("h_stored"); pad_stored = sem("pad_stored")
        filled = sem("filled"); const_done = sem("const_done"); tanh_done = sem("tanh_done"); gain_done = sem("gain_done")
        bk_spread = sem("bk_spread")
        m_done = sem("m_done"); vec_done = sem("vec_done"); m_hi_done = sem("m_hi_done"); m_lo_done = sem("m_lo_done")
        vec_evac = sem("vec_evac")
        st1_step = sem("st1_step"); rstd1_done = sem("rstd1_done"); a_ready = sem("a_ready")
        aT_done = sem("aT_done"); aT_hi_done = sem("aT_hi_done"); aT_lo_done = sem("aT_lo_done")
        cT_done = sem("cT_done"); cT_evac = sem("cT_evac")
        g_done = sem("g_done"); g_evac = sem("g_evac")
        scores_done = sem("scores_done"); peak_done = sem("peak_done"); neg_done = sem("neg_done")
        exp_done = sem("exp_done"); inv_done = sem("inv_done"); att_gain_done = sem("att_gain_done")
        pt_done = sem("pt_done"); pt_evac = sem("pt_evac"); pv_done = sem("pv_done"); x1_ready = sem("x1_ready")
        st2_step = sem("st2_step"); rstd2_done = sem("rstd2_done"); h_ready = sem("h_ready")
        hT_done = sem("hT_done"); hT_evac = sem("hT_evac"); logits_done = sem("logits_done"); mask_step = sem("mask_step")
        mask_ready = sem("mask_ready"); ranks_done = sem("ranks_done"); row_summed = sem("row_summed")
        ranks_read = sem("ranks_read"); terms_done = sem("terms_done"); logits_read = sem("logits_read")
        w_hi_done = sem("w_hi_done"); w_lo_done = sem("w_lo_done")
        count_done = sem("count_done"); route_step = sem("route_step"); slot_hot = sem("slot_hot"); blk_hot = sem("blk_hot")
        table_done = sem("table_done"); rows_known = sem("rows_known"); expert_known = sem("expert_known")
        row_in = [sem(f"row_in{u}") for u in range(BU)]
        xT_done = sem("xT_done"); xT_hi_done = sem("xT_hi_done"); xT_lo_done = sem("xT_lo_done")
        y_done = sem("y_done"); y_biased = sem("y_biased"); y_ready = sem("y_ready"); added = sem("added")
        gather_known = sem("gather_known"); add_known = sem("add_known")

        block = ctx.enter_context(nc.Block())

        @block.sync
        def _(sp):
            sp.dma_start(wq_sb[:, :, :], Wq.rearrange("(p k) x -> p k x", p=P)).then_inc(proj_in, 16)
            sp.dma_start(wk_sb[:, :, :], Wk.rearrange("(p k) x -> p k x", p=P)).then_inc(proj_in, 16)
            sp.dma_start(x_sb[:, 0], x_v[:, 0]).then_inc(x_first[0], 16)
            sp.dma_start(bqk[:, 0, :], bq.rearrange("(p k) -> p k", p=P)).then_inc(bias_in, 16)
            sp.dma_start(bqk[:, 1, :], bk.rearrange("(p k) -> p k", p=P)).then_inc(bias_in, 16)
            sp.dma_start(x_sb[:, 1], x_v[:, 1]).then_inc(x_first[1], 16)
            sp.dma_start(c_sb[:, 0], c_v[:, 0]).then_inc(c_first, 16)
            sp.dma_start(gates[:, 0:1], g_x[None, :].to_broadcast([P, 1])).then_inc(small_in, 16)
            sp.dma_start(gates[:, 1:2], g_f[None, :].to_broadcast([P, 1])).then_inc(small_in, 16)
            sp.dma_start(bg_sb[:, :], bg[None, :].to_broadcast([P, E])).then_inc(small_in, 16)
            sp.dma_start(wg_sb[:, :, :], Wg.rearrange("(k p) e -> p k e", p=P)).then_inc(small_in, 16)
            sp.dma_start(x_sb[:, 2], x_v[:, 2]).then_inc(x_first[2], 16)
            sp.dma_start(c_sb[:, 1], c_v[:, 1]).then_inc(c_in, 16)
            sp.dma_start(x_sb[:, 3], x_v[:, 3]).then_inc(x_in, 16)
            sp.dma_start(we_raw[:, 0:KC, :], we_v[:, 0:KC, :]).then_inc(w_in, 16)

            def store_x1(g):
                sp.wait_ge(x1_ready, TJ * g + TJ)
                sp.dma_start(out_v[:, ds(g, 1)], x_sb[:, ds(g % XR, 1)]).then_inc(x1_stored, 16)

            def store_h(g, first):
                sp.wait_ge(h_ready, TJ * g + TJ)
                if not first:
                    sp.wait_ge(h_stored, 16 * g)
                sp.dma_start(h_v[:, ds(g, 1)], h_sb[:, None]).then_inc(h_stored, 16)

            def load_x(g):
                sp.wait_ge(x1_stored, 16 * g + 16)
                sp.wait_ge(x_in, 16 * g + 16)
                sp.dma_start(x_sb[:, ds(g % XR, 1)], x_v[:, ds(g + XR, 1)]).then_inc(x_in, 16)

            def load_c(g, parity):
                sp.wait_ge(pv_done, TJ * g + TJ)
                sp.wait_ge(c_in, 16 * g + 16)
                sp.dma_start(c_sb[:, parity:parity + 1], c_v[:, ds(g + 2, 1)]).then_inc(c_in, 16)

            sp.dma_start(out[N:N + P, :], x.rearrange("b s d -> (b s) d")[0:P, :]).then_inc(pad_stored, 16)

            def load_w(e):
                sp.wait_ge(w_in, 16 * e)
                sp.dma_start(we_raw[:, ds(KC * e, KC), :], we_v[:, ds(KC * e, KC), :]).then_inc(w_in, 16)

            def group(g, parity, first):
                load_w(g + 1)
                store_x1(g)
                load_c(g, parity)
                store_h(g, first)
                load_x(g)

            group(0, 0, True)
            group(1, 1, False)
            with sp.Fori(1, GROUPS // 2 - 2) as i:
                for parity in range(2):
                    group(2 * i + parity, parity, False)
            sp.wait_ge(pad_stored, 16)
            for g in range(GROUPS - XR, GROUPS):
                if g + 1 < E:
                    load_w(g + 1)
                sp.wait_ge(x1_stored, 16 * g)
                store_x1(g)
                if g + 2 < GROUPS:
                    load_c(g, g % 2)
                store_h(g, False)
            sp.wait_ge(h_ready, TILES)
            sp.dma_start(be_sb[:, :, :], be[None, :, :].to_broadcast([P, E, D])).then_inc(be_in, 16)
            sp.wait_ge(added, 16 * BLOCKS)

        @block.scalar
        def _(act):
            def piece_hi(e, k):
                if k == 0:
                    act.wait_ge(w_in, 16 * e + 16)
                nc.scalar.copy(we_hi[:, ds(KC * e + k, 1), :], we_raw[:, ds(KC * e + k, 1), :]).then_inc(w_hi_done, 1)

            act.wait_ge(small_in, 64)
            nc.scalar.activation(tanh_g[:, :], gates[:, :], ACT.Tanh).then_inc(tanh_done, 1)
            for c in range(KC):
                act.wait_ge(m_done, c + 1)
                nc.scalar.copy(m_hi[:, c], m_ps[c][:, :]).then_inc(m_hi_done, 1)

            def evac_a(g, j):
                act.wait_ge(aT_done, TJ * g + j + 1)
                nc.scalar.copy(aT_hi[:, :, j * P:(j + 1) * P], tpv[a_tp[j]]).then_inc(aT_hi_done, 1)

            def evac_g(g, c):
                act.wait_ge(g_done, KC * g + c + 1)
                nc.scalar.activation(gT[:, c], gb[c % 2][:, 0:GT], ACT.Identity,
                                     bias=w_vec[:, c:c + 1]).then_inc(g_evac, 1)

            for j in range(TJ):
                evac_a(0, j)
            act.wait_ge(vec_evac, 1)
            for c in range(KC):
                evac_g(0, c)
            act.wait_ge(const_done, 1)

            def group(g, first, last, ahead):
                for j in range(TJ):
                    act.wait_ge(cT_done, TJ * g + j + 1)
                    nc.scalar.copy(cT[:, j], tpv[c_tp[j]]).then_inc(cT_evac, 1)
                for j in range(TJ):
                    act.wait_ge(neg_done, TJ * g + j + 1)
                    for r0 in (0, S):
                        rr = slice(r0, r0 + S)
                        e = nc.scalar.activation(p_sb[rr, j, r0:r0 + S], s_sb[rr, j], ACT.Exp,
                                                 bias=neg_peak[rr, j:j + 1], scale=SCALE,
                                                 accum_out=exp_sum[rr, j:j + 1])
                    e.then_inc(exp_done, 1)
                if not last:
                    evac_g(g + 1, 0)
                    evac_g(g + 1, 1)
                piece_hi(g, 0)
                if not first:
                    evac_h(g - 1)
                if not last:
                    evac_g(g + 1, 2)
                piece_hi(g, 1)
                for j in range(TJ):
                    act.wait_ge(pt_done, TJ * g + j + 1)
                    nc.scalar.copy(p_sb[:, j], sc[j][:, P:2 * P]).then_inc(pt_evac, 1)
                piece_hi(g, 2)
                if not last:
                    evac_g(g + 1, 3)
                if ahead:
                    for j in range(TJ):
                        evac_a(g + 2, j)
                piece_hi(g, 3)

            def evac_h(g):
                for j in range(TJ):
                    act.wait_ge(hT_done, TJ * g + j + 1)
                    nc.scalar.copy(hT[:, j], tpv[h_tp[j]]).then_inc(hT_evac, 1)

            for j in range(TJ):
                evac_a(1, j)
            group(0, True, False, True)
            with act.Fori(1, GROUPS - 2) as g:
                group(g, False, False, True)
            group(GROUPS - 2, False, False, False)
            group(GROUPS - 1, False, True, False)
            evac_h(GROUPS - 1)

            def block_hi(b, u):
                act.wait_ge(xT_done, b + 1)
                nc.scalar.copy(xT_hi[:, u], tbv[u]).then_inc(xT_hi_done, 1)

            with act.Fori(0, TURNS) as i:
                for u in range(BU):
                    block_hi(i * BU + u, u)
            for b in range(TURNS * BU, BLOCKS):
                block_hi(b, b % BU)

        @block.vector
        def _(dve):
            nc.vector.memset(half_neg[:, :], -0.5).then_inc(filled, 1)
            nc.vector.memset(ident[:, :], 1.0).then_inc(filled, 1)
            nc.vector.memset(ones_b[:, :], 1.0).then_inc(filled, 1)
            nc.vector.memset(earlier[:, :], 1.0).then_inc(filled, 1)
            nc.vector.memset(p_sb[:, :, :], 0.0).then_inc(const_done, 1)
            nc.vector.memset(ones8[:, :], 1.0)
            nc.vector.memset(taken[:, :], 0.0).then_inc(mask_step, 1)

            def stats1(q, g):
                for j in range(TJ):
                    nc.vector.bn_stats(st1[:, j], x_sb[:, ds(g % XR, 1), j]).then_inc(st1_step, 1)
                dve.drain()
                for j in range(TJ):
                    nc.vector.bn_aggr(mv1[:, j], st1[:, j]).then_inc(st1_step, 1)
                dve.wait_ge(st1_step, 5 * q + 4)
                nc.vector.tensor_scalar(ve1[:, :], mv1[:, :, 1], EPS, None, ALU.add).then_inc(st1_step, 1)

            def norm1(q, g, first):
                dve.wait_ge(rstd1_done, q + 1)
                for j in range(TJ):
                    if not first:
                        dve.wait_ge(aT_done, TJ * (q - 1) + j + 1)
                    nc.vector.tensor_scalar(a_sb[:, j], x_sb[:, ds(g % XR, 1), j], mv1[:, j, 0:1],
                                            rstd1[:, j:j + 1], ALU.subtract, ALU.mult).then_inc(a_ready, 1)

            def lo_a(g, j):
                dve.wait_ge(aT_hi_done, TJ * g + j + 1)
                t = slice(j * P, (j + 1) * P)
                nc.vector.tensor_tensor(aT_lo[:, :, t], tpv[a_tp[j]], aT_hi[:, :, t].bitcast(fp32),
                                        ALU.subtract).then_inc(aT_lo_done, 1)

            def row_terms(g, first):
                if first:
                    dve.wait_ge(a_ready, TJ)
                else:
                    dve.drain()
                for j in range(TJ):
                    nc.vector.scalar_tensor_tensor(a_sb[:, j], a_sb[:, j], 1.0, u_rows[:, :], ALU.mult, ALU.mult,
                                                   accum_out=row_sum[:, j:j + 1]).then_inc(row_summed, 1)
                dve.wait_ge(row_summed, TJ * g + TJ)
                nc.vector.tensor_scalar(row_term[:, :], row_sum[:, :], bb[:, 0:1], None, ALU.add).then_inc(terms_done, 1)

            def read_ranks(g):
                dve.wait_ge(ranks_done, g + 1)
                nc.vector.tensor_copy(rank[:, ds(TJ * g, TJ), :], rk_ps).then_inc(ranks_read, 1)

            dve.wait_ge(x_first[0], 16)
            stats1(0, 0)
            norm1(0, 0, True)
            dve.wait_ge(bias_in, 32)
            nc.vector.tensor_copy(bk_rows[:, :, :], bqk[:, 1, :, None].to_broadcast([P, KC, P])).then_inc(bk_spread, 1)
            for c in range(KC):
                dve.wait_ge(m_hi_done, c + 1)
                nc.vector.tensor_tensor(m_lo[:, c], m_ps[c][:, :], m_hi[:, c].bitcast(fp32),
                                        ALU.subtract).then_inc(m_lo_done, 1)
            dve.wait_ge(vec_done, 1)
            nc.vector.tensor_copy(bb[:, :], bb_ps)
            nc.vector.tensor_copy(u_rows[:, :], u_ps[:, :])
            nc.vector.tensor_copy(w_vec[:, :], w_ps).then_inc(vec_evac, 1)
            for j in range(TJ):
                lo_a(0, j)
            dve.wait_ge(x_first[1], 16)
            stats1(1, 1)
            dve.wait_ge(vec_evac, 1)
            row_terms(0, True)
            norm1(1, 1, False)
            dve.wait_ge(tanh_done, 1)
            nc.vector.tensor_scalar(ffn_gain[:, :], tanh_g[:, 1:2], 1.0 / TOPK, None, ALU.mult).then_inc(gain_done, 1)
            for j in range(TJ):
                lo_a(1, j)

            def soft(g, j):
                dve.wait_ge(scores_done, TJ * g + j + 1)
                if j == 0:
                    dve.wait_ge(terms_done, g + 1)
                for r0 in (0, S):
                    rr = slice(r0, r0 + S)
                    nc.vector.tensor_scalar(s_sb[rr, j], sc[j][rr, r0:r0 + S], row_term[rr, j:j + 1], None,
                                            ALU.add, ALU.max, accum_out=peak[rr, j:j + 1]).then_inc(peak_done, 1)
                dve.wait_ge(peak_done, 2 * (TJ * g + j + 1))
                nc.vector.tensor_scalar(neg_peak[:, j:j + 1], peak[:, j:j + 1], -SCALE, None,
                                        ALU.mult).then_inc(neg_done, 1)

            MS = 9

            def masks(g):
                b0 = MS * g + 1
                dve.wait_ge(logits_done, g + 1)
                nc.vector.tensor_tensor(logit[:, :, :], l_ps, bg_sb[:, None, :].to_broadcast([P, TJ, E]),
                                        ALU.add).then_inc(logits_read, 1)
                dve.drain()
                for j in range(TJ):
                    nc.vector.max(best[:, j], logit[:, j]).then_inc(mask_step, 1)
                dve.drain()
                for j in range(TJ):
                    nc.vector.max_index(best_at[:, j], best[:, j], logit[:, j]).then_inc(mask_step, 1)
                dve.wait_ge(mask_step, b0 + 4)
                nc.vector.tensor_copy(best_f[:, :, :], best_at[:, :, 0:TOPK]).then_inc(mask_step, 1)
                dve.wait_ge(mask_step, b0 + 5)
                for c in range(TOPK):
                    nc.vector.tensor_tensor(chosen[:, c, ds(TJ * g, TJ), :],
                                            iota_e[:, None, :].to_broadcast([P, TJ, E]),
                                            best_f[:, :, c:c + 1].to_broadcast([P, TJ, E]),
                                            ALU.is_equal).then_inc(mask_step, 1)
                dve.wait_ge(mask_step, b0 + 7)
                nc.vector.tensor_tensor(mask[:, :, :], chosen[:, 0, ds(TJ * g, TJ), :], chosen[:, 1, ds(TJ * g, TJ), :],
                                        ALU.add).then_inc(mask_ready, 1)

            def taken_more(g):
                b0 = MS * g + 1
                nc.vector.tensor_tensor(taken[:, :], taken[:, :], mask[:, 0], ALU.add).then_inc(mask_step, 1)
                dve.wait_ge(mask_step, b0 + 8)
                nc.vector.tensor_tensor(taken[:, :], taken[:, :], mask[:, 1], ALU.add).then_inc(mask_step, 1)

            def norm2(g, first):
                dve.wait_ge(rstd2_done, g + 1)
                if not first:
                    dve.wait_ge(hT_done, TJ * g)
                    dve.wait_ge(h_stored, 16 * g)
                for j in range(TJ):
                    nc.vector.tensor_scalar(h_sb[:, j], x_sb[:, ds(g % XR, 1), j], mv2[:, j, 0:1],
                                            rstd2[:, j:j + 1], ALU.subtract, ALU.mult).then_inc(h_ready, 1)

            def group(g, first, last, ahead, second=False):
                for j in range(TJ):
                    soft(g, j)
                if not first:
                    norm2(g - 1, second)
                if ahead:
                    if first:
                        dve.wait_ge(x_first[2], 16)
                    else:
                        dve.wait_ge(x_in, 16 * g)
                    stats1(g + 2, g + 2)
                if not last:
                    row_terms(g + 1, False)
                dve.wait_ge(exp_done, TJ * g + TJ)
                nc.vector.reciprocal(exp_inv[:, :], exp_sum[:, :]).then_inc(inv_done, 1)
                if ahead:
                    norm1(g + 2, g + 2, False)
                dve.wait_ge(inv_done, g + 1)
                nc.vector.tensor_scalar(att_gain[:, :], exp_inv[:, :], tanh_g[:, 0:1], None,
                                        ALU.mult).then_inc(att_gain_done, 1)
                if not first:
                    masks(g - 1)
                if ahead:
                    for j in range(TJ):
                        lo_a(g + 2, j)
                if not first:
                    read_ranks(g - 1)
                    taken_more(g - 1)
                dve.wait_ge(att_gain_done, g + 1)
                for j in range(TJ):
                    dve.wait_ge(pv_done, TJ * g + j + 1)
                    nc.vector.scalar_tensor_tensor(x_sb[:, ds(g % XR, 1), j], sc[j][:, :], att_gain[:, j:j + 1],
                                                   x_sb[:, ds(g % XR, 1), j], ALU.mult, ALU.add).then_inc(x1_ready, 1)
                dve.drain()
                for j in range(TJ):
                    nc.vector.bn_stats(st2[:, j], x_sb[:, ds(g % XR, 1), j]).then_inc(st2_step, 1)
                dve.drain()
                for j in range(TJ):
                    nc.vector.bn_aggr(mv2[:, j], st2[:, j]).then_inc(st2_step, 1)
                dve.wait_ge(st2_step, 5 * g + 4)
                nc.vector.tensor_scalar(ve2[:, :], mv2[:, :, 1], EPS, None, ALU.add).then_inc(st2_step, 1)

            group(0, True, False, True)
            group(1, False, False, True, second=True)
            with dve.Fori(2, GROUPS - 2) as g:
                group(g, False, False, True)
            group(GROUPS - 2, False, False, False)
            group(GROUPS - 1, False, True, False)
            norm2(GROUPS - 1, False)
            masks(GROUPS - 1)
            read_ranks(GROUPS - 1)
            taken_more(GROUPS - 1)

            dve.wait_ge(ranks_read, GROUPS)

            def after(n):
                dve.wait_ge(route_step, n)

            for c in range(TOPK):
                if c:
                    after(2)
                nc.vector.tensor_tensor(prod[:, :, :], rank[:, :, :], chosen[:, c], ALU.mult).then_inc(route_step, 1)
                after(2 * c + 1)
                nc.vector.tensor_reduce(rank_of[:, c], prod[:, :, :], AX.X, ALU.add).then_inc(route_step, 1)
            after(4)
            nc.vector.tensor_copy(rank_i[:, :, :], rank_of[:, :, :]).then_inc(route_step, 1)
            after(5)
            nc.vector.tensor_scalar(slot_i[:, :, :], rank_i[:, :, :], P - 1, None,
                                    ALU.bitwise_and).then_inc(route_step, 1)
            nc.vector.tensor_scalar(blk_i[:, :, :], rank_i[:, :, :], P.bit_length() - 1, None,
                                    ALU.arith_shift_right).then_inc(route_step, 1)
            after(7)
            nc.vector.tensor_copy(slot_of[:, :, :], slot_i[:, :, :]).then_inc(route_step, 1)
            nc.vector.tensor_copy(rank_blk[:, :, :], blk_i[:, :, :]).then_inc(route_step, 1)
            dve.wait_ge(count_done, 1)
            nc.vector.tensor_scalar(count_i[:, :], cnt_ps, float(P - 1), None, ALU.add).then_inc(route_step, 1)
            after(10)
            nc.vector.tensor_scalar(nblk_i[:, :], count_i[:, :], P.bit_length() - 1, None,
                                    ALU.arith_shift_right).then_inc(route_step, 1)
            after(11)
            nc.vector.tensor_copy(nblk[:, :], nblk_i[:, :]).then_inc(route_step, 1)
            after(12)
            nc.vector.tensor_tensor_scan(blk_end[:, :], ones8[:, :], nblk[:, :], 0.0, ALU.mult,
                                         ALU.add).then_inc(route_step, 1)
            after(13)
            nc.vector.tensor_tensor(blk_first[:, :], blk_end[:, :], nblk[:, :], ALU.subtract).then_inc(route_step, 1)
            for c in range(TOPK):
                after(14 + 2 * c)
                nc.vector.tensor_tensor(prod[:, :, :], chosen[:, c], blk_first[:, None, :].to_broadcast([P, TILES, E]),
                                        ALU.mult).then_inc(route_step, 1)
                after(15 + 2 * c)
                nc.vector.tensor_reduce(first_of[:, c], prod[:, :, :], AX.X, ALU.add).then_inc(route_step, 1)
            after(18)
            nc.vector.tensor_tensor(blk_of[:, :, :], rank_blk[:, :, :], first_of[:, :, :],
                                    ALU.add).then_inc(route_step, 1)
            after(19)
            for c in range(TOPK):
                for t in range(TILES):
                    n = c * TILES + t
                    nc.vector.tensor_scalar(in_slot[:, n], iota_p[:, :], slot_of[:, c, t:t + 1], None,
                                            ALU.is_equal).then_inc(slot_hot, 1)
                    nc.vector.tensor_scalar(in_blk[:, n], iota_blk[:, :], blk_of[:, c, t:t + 1],
                                            token1[:, t:t + 1], ALU.is_equal, ALU.mult).then_inc(blk_hot, 1)
            nc.vector.tensor_tensor(past[:, :, :], iota_blk[0:1, :, None].to_broadcast([1, BW, E]),
                                    blk_end[0:1, None, :].to_broadcast([1, BW, E]), ALU.is_ge).then_inc(route_step, 1)
            after(20)
            nc.vector.tensor_reduce(n_past[:, :], past[:, :, :], AX.X, ALU.add).then_inc(route_step, 1)
            after(21)
            nc.vector.tensor_scalar(expert_of[:, :], n_past[:, :], float(E - 1), None,
                                    ALU.min).then_inc(expert_known, 1)
            dve.wait_ge(table_done, 1)
            nc.vector.tensor_scalar(gather_row[:, :], table_ps, -1.0, 0.0, ALU.add, ALU.max).then_inc(rows_known, 1)
            nc.vector.tensor_scalar(pad_at[:, :], table_ps, 0.0, pad_row[:, 0:1], ALU.is_equal,
                                    ALU.mult).then_inc(route_step, 1)
            after(22)
            nc.vector.scalar_tensor_tensor(add_row[:, :], table_ps, -1.0, pad_at[:, :], ALU.add,
                                           ALU.add).then_inc(rows_known, 1)

            dve.wait_ge(be_in, 16)
            dve.wait_ge(gain_done, 1)
            dve.wait_ge(expert_known, 1)

            def block_lo(b, u):
                dve.wait_ge(xT_hi_done, b + 1)
                nc.vector.tensor_tensor(xT_lo[:, u], tbv[u], xT_hi[:, u].bitcast(fp32),
                                        ALU.subtract).then_inc(xT_lo_done, 1)

            def block_y(b, u, first):
                e = dve.value_load(expert_of[0:1, ds(b, 1)], min_val=0, max_val=E - 1)
                dve.wait_ge(y_done, b + 1)
                nc.vector.tensor_tensor(y_raw[:, u], yb[u][:, :], be_sb[:, ds(e, 1), :], ALU.add).then_inc(y_biased, 1)
                if not first:
                    dve.wait_ge(added, 16 * (b - BU + 1))
                dve.wait_ge(y_biased, b + 1)
                nc.vector.tensor_scalar(y_sb[:, u], y_raw[:, u], 0.0, ffn_gain[:, 0:1], ALU.max,
                                        ALU.mult).then_inc(y_ready, 1)

            block_lo(0, 0)
            for u in range(BU):
                block_lo(u + 1, (u + 1) % BU)
                block_y(u, u, True)
            with dve.Fori(1, TURNS) as i:
                for u in range(BU):
                    block_lo(i * BU + u + 1, (u + 1) % BU)
                    block_y(i * BU + u, u, False)
            for b in range(TURNS * BU, BLOCKS):
                if b + 1 < BLOCKS:
                    block_lo(b + 1, (b + 1) % BU)
                block_y(b, b % BU, False)

        @block.gpsimd
        def _(pool):
            def piece_lo(e, k):
                n = KC * e + k
                pool.wait_ge(w_hi_done, n + 1)
                nc.gpsimd.tensor_tensor(we_lo[:, ds(n, 1), :], we_raw[:, ds(n, 1), :],
                                        we_hi[:, ds(n, 1), :].bitcast(fp32), ALU.subtract).then_inc(w_lo_done, 1)

            def rstd(q, steps, var_eps, rstd_, done):
                pool.wait_ge(steps, 5 * q + 5)
                nc.gpsimd.tensor_tensor(rstd_[:, :], var_eps[:, :], half_neg[:, :], ALU.pow).then_inc(done, 1)

            nc.gpsimd.memset(gate[:, :], 0.0)
            pool.wait_ge(filled, 4)
            nc.gpsimd.affine_select(ident[:, :], ident[:, :], [[1, P]], ALU.is_equal, 0.0, base=0,
                                    channel_multiplier=-1).then_inc(const_done, 1)
            nc.gpsimd.affine_select(earlier[:, :], earlier[:, :], [[1, P]], ALU.is_gt, 0.0, base=0,
                                    channel_multiplier=-1).then_inc(const_done, 1)
            rstd(0, st1_step, ve1, rstd1, rstd1_done)
            nc.gpsimd.iota(iota_e[:, :], [[1, E]], base=0, channel_multiplier=0,
                           allow_small_or_imprecise_dtypes=True).then_inc(const_done, 1)
            nc.gpsimd.iota(iota_p[:, :], [[1, P]], base=0, channel_multiplier=0,
                           allow_small_or_imprecise_dtypes=True).then_inc(const_done, 1)
            nc.gpsimd.iota(iota_blk[:, :], [[1, BW]], base=0, channel_multiplier=0,
                           allow_small_or_imprecise_dtypes=True).then_inc(const_done, 1)
            nc.gpsimd.iota(token1[:, :], [[P, TILES]], base=1, channel_multiplier=1,
                           allow_small_or_imprecise_dtypes=True).then_inc(const_done, 1)
            nc.gpsimd.iota(pad_row[:, :], [[1, 1]], base=N + 1, channel_multiplier=1,
                           allow_small_or_imprecise_dtypes=True).then_inc(const_done, 1)
            rstd(1, st1_step, ve1, rstd1, rstd1_done)

            def group(g, ahead):
                if ahead:
                    rstd(g + 2, st1_step, ve1, rstd1, rstd1_done)
                for k in range(KC):
                    piece_lo(g, k)
                rstd(g, st2_step, ve2, rstd2, rstd2_done)

            with pool.Fori(0, GROUPS - 2) as g:
                group(g, True)
            group(GROUPS - 2, False)
            group(GROUPS - 1, False)

            def gather(b, u):
                pool.indirect_dma_start(out=rows[:, u, :], out_offset=None, in_=h_dram,
                                        in_offset=bass.IndirectOffsetOnAxis(ap=gather_at[:, u:u + 1], axis=0)
                                        ).then_inc(row_in[u], 16)

            def add(b, u):
                pool.indirect_dma_start(out=out, out_offset=bass.IndirectOffsetOnAxis(ap=add_at[:, u:u + 1], axis=0),
                                        in_=y_sb[:, u, :], in_offset=None, compute_op=ALU.add).then_inc(added, 16)

            pool.wait_ge(rows_known, 1)
            for u in range(BU):
                nc.gpsimd.tensor_copy(gather_at[:, u:u + 1], gather_row[:, u:u + 1]).then_inc(gather_known, 1)
            pool.wait_ge(gather_known, BU)
            pool.wait_ge(h_stored, 16 * GROUPS)
            for u in range(BU):
                gather(u, u)
            pool.wait_ge(rows_known, 2)
            pool.wait_ge(x1_stored, 16 * GROUPS)
            pool.wait_ge(pad_stored, 16)

            def turn(b, u, first, more):
                v = (u + 1) % BU
                nc.gpsimd.tensor_copy(add_at[:, u:u + 1], add_row[:, ds(b, 1)]).then_inc(add_known, 1)
                if more:
                    pool.wait_ge(xT_done, b + 2)
                    nc.gpsimd.tensor_copy(gather_at[:, v:v + 1], gather_row[:, ds(b + BU + 1, 1)]).then_inc(gather_known, 1)
                    pool.wait_ge(gather_known, b + BU + 2)
                pool.wait_ge(add_known, b + 1)
                pool.wait_ge(y_ready, b + 1)
                if not first:
                    pool.wait_ge(added, 16 * b)
                nc.gpsimd.tensor_tensor(gate[:, :], gate[:, :], gate[:, :], ALU.add)
                add(b, u)
                if more:
                    gather(b + BU + 1, v)

            pool.wait_ge(xT_done, 1)
            nc.gpsimd.tensor_copy(gather_at[:, 0:1], gather_row[:, BU:BU + 1]).then_inc(gather_known, 1)
            pool.wait_ge(gather_known, BU + 1)
            gather(BU, 0)
            for u in range(BU):
                turn(u, u, u == 0, True)
            with pool.Fori(1, TURNS - 1) as i:
                for u in range(BU):
                    turn(i * BU + u, u, False, True)
            for b in range((TURNS - 1) * BU, BLOCKS):
                turn(b, b % BU, False, b + BU + 1 < BLOCKS)
            pool.wait_ge(added, 16 * BLOCKS)

        @block.tensor
        def _(pe):
            def chunks4(dst, src, done):
                for k in range(KC):
                    t = nc.tensor.transpose(dst[:, k * P:(k + 1) * P], src(k), ident[:, :])
                t.then_inc(done, 1)

            def product3(dst, k3, k_hi, k_lo, rhs_hi, rhs_lo):
                for k in range(k3):
                    nc.tensor.matmul(dst, k_hi(k), rhs_hi(k), start=(k == 0), stop=False)
                    nc.tensor.matmul(dst, k_hi(k), rhs_lo(k), start=False, stop=False)
                    last = nc.tensor.matmul(dst, k_lo(k), rhs_hi(k), start=False, stop=(k == k3 - 1))
                return last

            pe.wait_ge(proj_in, 32)
            for c in range(KC):
                for k in range(KC):
                    m = nc.tensor.matmul(m_ps[c][:, :], wq_sb[:, k, c * P:(c + 1) * P], wk_sb[:, k, :],
                                         start=(k == 0), stop=(k == KC - 1))
                m.then_inc(m_done, 1)
            pe.wait_ge(bias_in, 32)
            for c in range(KC):
                for k in range(KC):
                    nc.tensor.matmul(w_ps[:, c:c + 1], wk_sb[:, k, c * P:(c + 1) * P], bqk[:, 0, k:k + 1],
                                     start=(k == 0), stop=(k == KC - 1))
            pe.wait_ge(bk_spread, 1)
            for k in range(KC):
                nc.tensor.matmul(bb_ps, bk_rows[:, k, :], bqk[:, 0, k:k + 1], start=(k == 0), stop=(k == KC - 1))
            for k in range(KC):
                m = nc.tensor.matmul(u_ps[:, :], bk_rows[:, k, :], wq_sb[:, k, :], start=(k == 0), stop=(k == KC - 1))
            m.then_inc(vec_done, 1)

            def transpose_a(g, j):
                pe.wait_ge(a_ready, TJ * g + j + 1)
                chunks4(tp[a_tp[j]], lambda k: a_sb[:, j, k * P:(k + 1) * P], aT_done)

            def product_g(g, c, first):
                if not first or c >= 2:
                    pe.wait_ge(g_evac, KC * g + c - 1)
                cc = slice(c * P, (c + 1) * P)
                product3(gb[c % 2][:, 0:GT], KC, lambda k: m_hi[:, k, cc], lambda k: m_lo[:, k, cc],
                         lambda k: aT_hi[:, k, :], lambda k: aT_lo[:, k, :]).then_inc(g_done, 1)

            pe.wait_ge(const_done, 2)
            pe.wait_ge(vec_evac, 1)
            for j in range(TJ):
                transpose_a(0, j)
            pe.wait_ge(m_lo_done, KC)
            pe.wait_ge(aT_lo_done, TJ)
            for c in range(KC):
                product_g(0, c, True)
            for j in range(TJ):
                transpose_a(1, j)

            def transpose_h(g):
                for j in range(TJ):
                    pe.wait_ge(h_ready, TJ * g + j + 1)
                    chunks4(tp[h_tp[j]], lambda k: h_sb[:, j, k * P:(k + 1) * P], hT_done)

            def logits(g, first):
                pe.wait_ge(hT_evac, TJ * g + TJ)
                if not first:
                    pe.wait_ge(ranks_read, g)
                for j in range(TJ):
                    for k in range(KC):
                        m = nc.tensor.matmul(l_ps[:, j], hT[:, j, k, :], wg_sb[:, k, :], start=(k == 0), stop=(k == KC - 1))
                m.then_inc(logits_done, 1)

            def ranks(g):
                pe.wait_ge(mask_ready, g + 1)
                pe.wait_ge(logits_read, g + 1)
                nc.tensor.matmul(rk_ps[:, 0], earlier[:, :], mask[:, 0], start=True, stop=False)
                m = nc.tensor.matmul(rk_ps[:, 0], ones_b[:, :], taken[:, :], start=False, stop=True)
                nc.tensor.matmul(rk_ps[:, 1], earlier[:, :], mask[:, 1], start=True, stop=False)
                nc.tensor.matmul(rk_ps[:, 1], ones_b[:, :], mask[:, 0], start=False, stop=False)
                return nc.tensor.matmul(rk_ps[:, 1], ones_b[:, :], taken[:, :], start=False, stop=True)

            def group(g, parity, first, last, ahead, second=False):
                if first:
                    pe.wait_ge(c_first, 16)
                else:
                    pe.wait_ge(c_in, 16 * g)
                if not last:
                    pe.wait_ge(aT_lo_done, TJ * (g + 1) + 1)
                for j in range(TJ):
                    chunks4(tp[c_tp[j]], lambda k: c_sb[:, parity, j, k * P:(k + 1) * P], cT_done)
                pe.wait_ge(g_evac, KC * g + KC)
                for j in range(TJ):
                    pe.wait_ge(cT_evac, TJ * g + j + 1)
                    if not first:
                        pe.wait_ge(x1_ready, TJ * (g - 1) + j + 1)
                    for k in range(KC):
                        m = nc.tensor.matmul(sc[j][:, 0:P], gT[:, k, j * P:(j + 1) * P], cT[:, j, k, :],
                                             start=(k == 0), stop=(k == KC - 1))
                    m.then_inc(scores_done, 1)
                if not last:
                    pe.wait_ge(aT_lo_done, TJ * (g + 1) + TJ)
                    product_g(g + 1, 0, False)
                    product_g(g + 1, 1, False)
                if not first:
                    transpose_h(g - 1)
                if not last:
                    product_g(g + 1, 2, False)
                if not first:
                    logits(g - 1, second)
                for j in range(TJ):
                    pe.wait_ge(exp_done, TJ * g + j + 1)
                    nc.tensor.transpose(sc[j][:, P:2 * P], p_sb[:, j], ident[:, :]).then_inc(pt_done, 1)
                if not last:
                    product_g(g + 1, 3, False)
                if ahead:
                    for j in range(TJ):
                        transpose_a(g + 2, j)
                if not first:
                    ranks(g - 1).then_inc(ranks_done, 1)
                for j in range(TJ):
                    pe.wait_ge(pt_evac, TJ * g + j + 1)
                    nc.tensor.matmul(sc[j][:, :], p_sb[:, j], c_sb[:, parity, j, :], start=True, stop=True).then_inc(pv_done, 1)

            pe.wait_ge(small_in, 64)
            group(0, 0, True, False, True)
            group(1, 1, False, False, True, second=True)
            with pe.Fori(1, GROUPS // 2 - 1) as i:
                for parity in range(2):
                    group(2 * i + parity, parity, False, False, True)
            group(GROUPS - 2, 0, False, False, False)
            group(GROUPS - 1, 1, False, True, False)
            transpose_h(GROUPS - 1)
            logits(GROUPS - 1, False)
            ranks(GROUPS - 1).then_inc(ranks_done, 1)
            pe.wait_ge(ranks_read, GROUPS)
            pe.wait_ge(mask_step, 9 * GROUPS + 1)
            nc.tensor.matmul(cnt_ps, ones_b[:, :], taken[:, :], start=True, stop=True).then_inc(count_done, 1)
            for n in range(TOPK * TILES):
                pe.wait_ge(slot_hot, n + 1)
                pe.wait_ge(blk_hot, n + 1)
                m = nc.tensor.matmul(table_ps, in_slot[:, n], in_blk[:, n], start=(n == 0), stop=(n == TOPK * TILES - 1))
            m.then_inc(table_done, 1)

            def transpose_rows(b, u, arrived):
                pe.wait_ge(row_in[u], arrived)
                chunks4(tb[u], lambda k: rows[:, u, k * P:(k + 1) * P], xT_done)

            def block_product(b, u, first):
                e = pe.value_load(expert_of[0:1, ds(b, 1)], min_val=0, max_val=E - 1)
                pe.wait_ge(xT_lo_done, b + 1)
                if not first:
                    pe.wait_ge(y_biased, b - BU + 1)
                product3(yb[u][:, :], KC, lambda k: xT_hi[:, u, k, :], lambda k: xT_lo[:, u, k, :],
                         lambda k: we_hi[:, ds(e * KC + k, 1), :], lambda k: we_lo[:, ds(e * KC + k, 1), :]).then_inc(y_done, 1)

            pe.wait_ge(expert_known, 1)
            pe.wait_ge(w_lo_done, E * KC)
            transpose_rows(0, 0, 16)
            for u in range(BU):
                transpose_rows(u + 1, (u + 1) % BU, 16 * ((u + 1) // BU) + 16)
                block_product(u, u, True)
            with pe.Fori(1, TURNS) as i:
                for u in range(BU):
                    transpose_rows(i * BU + u + 1, (u + 1) % BU, 16 * i + 16 * ((u + 1) // BU) + 16)
                    block_product(i * BU + u, u, False)
            for b in range(TURNS * BU, BLOCKS):
                if b + 1 < BLOCKS:
                    transpose_rows(b + 1, (b + 1) % BU, 16 * ((b + 1) // BU) + 16)
                block_product(b, b % BU, False)


_INS = ["x", "ctx_4096", "g_xattn", "g_ffn", "L0_xattn_Wq", "L0_xattn_bq", "L0_xattn_Wk", "L0_xattn_bk",
        "L0_ffn_W_gate", "L0_ffn_b_gate", "L0_ffn_W_e", "L0_ffn_b_e"]


def kernel(**inputs):
    import numpy as _np
    import concourse.bacc as _bacc
    from concourse import mybir as _mybir
    from concourse.bass_utils import run_bass_kernel_spmd as _run

    nc = _bacc.Bacc("TRN2", target_bir_lowering=False, num_devices=1)
    arrays, args = {}, []
    for name in _INS:
        a = _np.ascontiguousarray(inputs[name])
        arrays[f"in_{name}"] = a
        args.append(nc.dram_tensor(f"in_{name}", a.shape, _mybir.dt.from_np(a.dtype), kind="ExternalInput").ap())
    out = nc.dram_tensor("out_rows", (N + P, D), _mybir.dt.float32, kind="ExternalOutput").ap()
    gated_xattn_moe(nc, *args, out)
    r = _run(nc, [arrays], core_ids=[0])
    return _np.asarray(r.results[0]["out_rows"])[:N].reshape(B, S, D)
```

```python
import concourse.bass as bass
from concourse import mybir
from contextlib import ExitStack

fp32 = mybir.dt.float32
fp32r = mybir.dt.float32r
bf16 = mybir.dt.bfloat16
i32 = mybir.dt.int32
u32 = mybir.dt.uint32
ALU = mybir.AluOpType
ACT = mybir.ActivationFunctionType
AX = mybir.AxisListType
ds = bass.ds

P = 128
B, S, D = 32, 64, 512
E, TOPK = 8, 2
KC = D // P
N = B * S
TJ = 2
GT = TJ * P
GROUPS = N // GT
TILES = N // P
XR = 4
BLOCKS = (TOPK * N - E) // P + E
BU = 4
TURNS = (BLOCKS - 1) // BU
AHEAD = GROUPS - 3
EARLY = (AHEAD * TOPK * GT - E * (P - 1)) // P // BU * BU
CPE = N // P
COLS = (E + 1) * CPE
PADS = (1 + BU) * P
XU = 2
SCALE = float(D) ** -0.5
EPS = 1e-5
MS, SS = 8, 5
CONSTS = 4 + BU - 1
assert GROUPS % 2 == 0 and BLOCKS > TURNS * BU and EARLY >= 3 * BU and BLOCKS - TOPK * N // P < CPE
assert GROUPS == E


def gated_xattn_moe(nc, x, ctx_, g_x, g_f, Wq, bq, Wk, bk, Wg, bg, We, be, out):
    x_v = x.rearrange("b s d -> (b s) d").rearrange("(g j p) d -> p g j d", j=TJ, p=P)
    c_v = ctx_.rearrange("b s d -> (b s) d").rearrange("(g j p) d -> p g j d", j=TJ, p=P)
    out_v = out[0:N, :].rearrange("(g j p) d -> p g j d", j=TJ, p=P)
    we_v = We.rearrange("e (k p) h -> p (e k) h", p=P)
    h_dram = nc.dram_tensor("h_dram", [N + PADS, D], fp32, kind="Internal").ap()
    ids_dram = nc.dram_tensor("ids_dram", [P * COLS, 1], i32, kind="Internal").ap()
    ids_v = ids_dram.rearrange("(p c) o -> p (c o)", p=P)
    h_v = h_dram[0:N, :].rearrange("(g j p) d -> p g j d", j=TJ, p=P)

    ctx = ExitStack()
    with ctx:
        def sb_in(stack, name, shape, dt):
            return stack.enter_context(nc.sbuf_tensor(name, shape, dt))

        def sem(name):
            return ctx.enter_context(nc.semaphore(name))

        def sb(name, shape, dt):
            return sb_in(ctx, name, shape, dt)

        we_hi = sb("we_hi", [P, E * KC, D], fp32r)
        loading = ExitStack()
        we_raw = sb_in(loading, "we_raw", [P, E * KC, D], fp32)
        loading.close()
        we_lo = sb("we_lo", [P, E * KC, D], fp32r)
        ident = sb("ident", [P, P], fp32)
        earlier = sb("earlier", [P, P], bf16)
        ones_b = sb("ones_b", [P, P], bf16)
        ones8 = sb("ones8", [P, E], fp32)
        iota_e = sb("iota_e", [P, E], fp32)
        iota_b = sb("iota_b", [1, BLOCKS], fp32)
        token = sb("token", [P, TILES], i32)
        half_neg = sb("half_neg", [P, TJ], fp32)
        gates = sb("gates", [P, 2], fp32)
        tanh_g = sb("tanh_g", [P, 2], fp32)
        ffn_gain = sb("ffn_gain", [P, 1], fp32)
        chosen = sb("chosen", [P, TJ, TOPK, E], bf16)
        taken = sb("taken", [P, E], bf16)
        ids = sb("ids", [P, 2, COLS], i32)
        gather_at = sb("gather_at", [P, BU], i32)
        add_at = sb("add_at", [P, BU], i32)
        gate = sb("gate", [1, 2], fp32)
        expert_of = sb("expert_of", [1, BLOCKS], i32)
        column_of = sb("column_of", [1, BLOCKS], i32)
        other = sb("other", [1, BU - 1, BLOCKS], fp32)
        added_base = sb("added_base", [1, BU - 1, BU * (BLOCKS // BU + 2)], fp32)
        added_need = sb("added_need", [1, BU - 1, BLOCKS], i32)
        slot_prod = sb("slot_prod", [P, TJ, TOPK, E], fp32)
        rank_of = sb("rank_of", [P, TJ, TOPK], fp32)
        place0 = sb("place0", [P, TJ, TOPK], fp32)
        place = sb("place", [P, TJ, TOPK], fp32)
        place_i = sb("place_i", [P, TJ, TOPK], i32)
        slot_i = sb("slot_i", [P, TJ, TOPK], i32)
        slot_f = sb("slot_f", [P, TJ, TOPK], fp32)
        id_at = sb("id_at", [P, TJ * TOPK], i32)
        early_id_at = sb("early_id_at", [P, TJ * TOPK], i32)
        early_token_at = sb("early_token_at", [P, TJ], i32)
        token_at = sb("token_at", [P, TJ], i32)
        count_i = sb("count_i", [1, E], i32)
        nblk_i = sb("nblk_i", [1, E], i32)
        nblk = sb("nblk", [1, E], fp32)
        blk_end = sb("blk_end", [1, E], fp32)
        blk_first = sb("blk_first", [1, E], fp32)
        early_end = sb("early_end", [1, E], fp32)
        early_first = sb("early_first", [1, E], fp32)
        early = sb("early", [1, E + 1], fp32)
        stride = sb("stride", [1, E], fp32)
        stride2 = sb("stride2", [1, E], fp32)
        past = sb("past", [1, BLOCKS, E], bf16)
        skip = sb("skip", [1, BLOCKS, E], bf16)
        n_past = sb("n_past", [1, BLOCKS], fp32)
        skipped = sb("skipped", [1, BLOCKS], fp32)
        column0 = sb("column0", [1, BLOCKS], fp32)

        s1 = ExitStack()
        x_sb = sb_in(s1, "x_sb", [P, XR, TJ, D], fp32)
        s0 = ExitStack()
        wq_sb = sb_in(s0, "wq_sb", [P, KC, D], fp32)
        wk_sb = sb_in(s0, "wk_sb", [P, KC, D], fp32)
        sb_in(s0, "loaded_meanwhile", [P, 7 * KC, GT], fp32)
        bqk = sb_in(s0, "bqk", [P, 2, KC], fp32)
        bk_rows = sb_in(s0, "bk_rows", [P, KC, P], fp32)
        s0.close()
        aT_hi = sb_in(s1, "aT_hi", [P, KC, GT], fp32r)
        aT_lo = sb_in(s1, "aT_lo", [P, KC, GT], fp32r)
        gT = sb_in(s1, "gT", [P, KC, GT], fp32)
        cT = sb_in(s1, "cT", [P, TJ, KC, P], fp32)
        a_sb = sb_in(s1, "a_sb", [P, TJ, D], fp32)
        c_sb = sb_in(s1, "c_sb", [P, 2, TJ, D], fp32)
        m_hi = sb_in(s1, "m_hi", [P, KC, D], fp32r)
        m_lo = sb_in(s1, "m_lo", [P, KC, D], fp32r)
        hT = sb_in(s1, "hT", [P, TJ, KC, P], fp32)
        h_sb = sb_in(s1, "h_sb", [P, TJ, D], fp32)
        wg_sb = sb_in(s1, "wg_sb", [P, KC, E], fp32)
        bg_sb = sb_in(s1, "bg_sb", [P, E], fp32)
        w_vec = sb_in(s1, "w_vec", [P, KC], fp32)
        u_rows = sb_in(s1, "u_rows", [P, D], fp32)
        bb = sb_in(s1, "bb", [P, 1], fp32)
        s_sb = sb_in(s1, "s_sb", [P, TJ, S], fp32)
        p_sb = sb_in(s1, "p_sb", [P, TJ, P], fp32)
        row_sum = sb_in(s1, "row_sum", [P, TJ], fp32)
        row_term = sb_in(s1, "row_term", [P, TJ], fp32)
        peak = sb_in(s1, "peak", [P, TJ], fp32)
        neg_peak = sb_in(s1, "neg_peak", [P, TJ], fp32)
        exp_sum = sb_in(s1, "exp_sum", [P, TJ], fp32)
        exp_inv = sb_in(s1, "exp_inv", [P, TJ], fp32)
        att_gain = sb_in(s1, "att_gain", [P, TJ], fp32)
        st1 = sb_in(s1, "st1", [P, TJ, 6], fp32)
        mv1 = sb_in(s1, "mv1", [P, TJ, 2], fp32)
        neg_mean1 = sb_in(s1, "neg_mean1", [P, TJ], fp32)
        shift1 = sb_in(s1, "shift1", [P, TJ], fp32)
        ve1 = sb_in(s1, "ve1", [P, TJ], fp32)
        rstd1 = sb_in(s1, "rstd1", [P, TJ], fp32)
        st2 = sb_in(s1, "st2", [P, TJ, 6], fp32)
        mv2 = sb_in(s1, "mv2", [P, TJ, 2], fp32)
        ve2 = sb_in(s1, "ve2", [P, TJ], fp32)
        rstd2 = sb_in(s1, "rstd2", [P, TJ], fp32)
        logit = sb_in(s1, "logit", [P, TJ, E], fp32)
        best = sb_in(s1, "best", [P, TJ, E], fp32)
        best_at = sb_in(s1, "best_at", [P, TJ, E], u32)
        best_f = sb_in(s1, "best_f", [P, TJ, TOPK], fp32)
        mask = sb_in(s1, "mask", [P, TJ, E], bf16)
        s1.close()
        s2 = ExitStack()
        y_sb = sb_in(s2, "y_sb", [P, BU, D], fp32)
        sb_in(s2, "x_kept", [P, 2 * TJ, D], fp32)
        rows = sb_in(s2, "rows", [P, BU, D], fp32)
        y_raw = sb_in(s2, "y_raw", [P, BU, D], fp32)
        xT_hi = sb_in(s2, "xT_hi", [P, XU, KC, P], fp32r)
        xT_lo = sb_in(s2, "xT_lo", [P, XU, KC, P], fp32r)
        sb_in(s2, "c_kept", [P, TJ, D], fp32)
        be_sb = sb_in(s2, "be_sb", [P, E, D], fp32)
        s2.close()

        tp = [ctx.enter_context(nc.psum_tensor(f"tp{i}", [P, D], fp32)) for i in range(3)]
        gb = [ctx.enter_context(nc.psum_tensor(f"gb{i}", [P, D], fp32)) for i in range(2)]
        sc = [ctx.enter_context(nc.psum_tensor(f"sc{i}", [P, D], fp32)) for i in range(2)]
        mb = ctx.enter_context(nc.psum_tensor("mb", [P, D], fp32))
        m_ps = [gb[0], gb[1], sc[0], sc[1]]
        w_ps, bb_ps, u_ps = mb[:, 0:KC], mb[:, KC:KC + 1], tp[1]
        l_ps = mb[:, 32:32 + TJ * E].rearrange("p (j e) -> p j e", e=E)
        rk_ps = mb[:, 64:64 + TJ * E].rearrange("p (j e) -> p j e", e=E)
        cnt_full_ps = mb[:, 96:96 + E]
        cnt_ps = mb[0:1, 96:96 + E]
        tb = [tp[2], tp[0]]
        yb = [gb[0], gb[1], sc[0], sc[1]]
        c_tp, a_tp = (1, 0), (0, 2)
        former_h = (tp[1], tp[2])
        last_h = (tp[1], sc[1])
        tpv = [t[:, :].rearrange("p (k t) -> p k t", k=KC) for t in tp]
        former_hv = [t[:, :].rearrange("p (k t) -> p k t", k=KC) for t in former_h]
        last_hv = [t[:, :].rearrange("p (k t) -> p k t", k=KC) for t in last_h]
        tbv = [t[:, :].rearrange("p (k t) -> p k t", k=KC) for t in tb]

        proj_in = [sem(f"proj_in{k}") for k in range(KC)]
        bias_in = sem("bias_in")
        small_in = sem("small_in")
        x_first = [sem(f"x_first{g}") for g in range(3)]
        x_in = sem("x_in")
        c_first = sem("c_first")
        c_in = sem("c_in")
        w_first = [sem(f"w_first{e}") for e in range(2)]
        w_in = sem("w_in")
        be_in = sem("be_in")
        ids_in = sem("ids_in")
        x1_stored = sem("x1_stored")
        h_stored = sem("h_stored")
        pad_stored = sem("pad_stored")
        h_pad_stored = sem("h_pad_stored")
        empty_stored = sem("empty_stored")
        ids_stored = sem("ids_stored")
        filled = sem("filled")
        ident_done = sem("ident_done")
        const_done = sem("const_done")
        ids_filled = sem("ids_filled")
        tanh_done = sem("tanh_done")
        gain_done = sem("gain_done")
        bk_spread = sem("bk_spread")
        m_done = sem("m_done")
        m_hi_done = sem("m_hi_done")
        m_lo_done = sem("m_lo_done")
        u_done = sem("u_done")
        vec_done = sem("vec_done")
        vec_evac = sem("vec_evac")
        w_hi_done = sem("w_hi_done")
        w_lo_done = sem("w_lo_done")
        st1_step = sem("st1_step")
        rstd1_done = sem("rstd1_done")
        a_ready = sem("a_ready")
        aT_done = sem("aT_done")
        aT_hi_done = sem("aT_hi_done")
        aT_lo_done = sem("aT_lo_done")
        row_summed = sem("row_summed")
        terms_done = sem("terms_done")
        g_done = sem("g_done")
        g_evac = sem("g_evac")
        cT_done = sem("cT_done")
        cT_evac = sem("cT_evac")
        scores_done = sem("scores_done")
        peak_done = sem("peak_done")
        neg_done = sem("neg_done")
        exp_done = sem("exp_done")
        inv_done = sem("inv_done")
        att_gain_done = sem("att_gain_done")
        pt_done = sem("pt_done")
        pt_evac = sem("pt_evac")
        pv_done = sem("pv_done")
        x1_ready = sem("x1_ready")
        st2_step = sem("st2_step")
        rstd2_done = sem("rstd2_done")
        h_ready = sem("h_ready")
        hT_done = sem("hT_done")
        hT_evac = sem("hT_evac")
        logits_done = sem("logits_done")
        logits_read = sem("logits_read")
        mask_step = sem("mask_step")
        mask_ready = sem("mask_ready")
        ranks_done = sem("ranks_done")
        ranks_read = sem("ranks_read")
        slot_step = sem("slot_step")
        id_known = sem("id_known")
        token_copied = sem("token_copied")
        count_done = sem("count_done")
        route_step = sem("route_step")
        lists_known = sem("lists_known")
        other_done = sem("other_done")
        others_known = sem("others_known")
        first_known = sem("first_known")
        gather_known = sem("gather_known")
        add_known = sem("add_known")
        row_in = [sem(f"row_in{u}") for u in range(BU)]
        xT_done = sem("xT_done")
        xT_hi_done = sem("xT_hi_done")
        xT_lo_done = sem("xT_lo_done")
        y_done = sem("y_done")
        y_biased = sem("y_biased")
        y_ready = sem("y_ready")
        rows_free = sem("rows_free")
        gated = sem("gated")
        added = [sem(f"added{u}") for u in range(BU)]

        block = ctx.enter_context(nc.Block())

        flat_ids = ids[:, :, :].rearrange("p t c -> p (t c)")

        def yb_of(b, u):
            return yb[u % 2] if isinstance(b, int) and b < BU else yb[u]

        @block.sync
        def _(sp):
            for k in range(KC):
                sp.dma_start(wq_sb[:, k], Wq.rearrange("(p k) x -> p k x", p=P)[:, k]).then_inc(proj_in[k], 16)
                sp.dma_start(wk_sb[:, k], Wk.rearrange("(p k) x -> p k x", p=P)[:, k]).then_inc(proj_in[k], 16)
            sp.dma_start(x_sb[:, 0], x_v[:, 0]).then_inc(x_first[0], 16)
            sp.dma_start(bqk[:, 0, :], bq.rearrange("(p k) -> p k", p=P)).then_inc(bias_in, 16)
            sp.dma_start(bqk[:, 1, :], bk.rearrange("(p k) -> p k", p=P)).then_inc(bias_in, 16)
            sp.dma_start(x_sb[:, 1], x_v[:, 1]).then_inc(x_first[1], 16)
            sp.dma_start(c_sb[:, 0], c_v[:, 0]).then_inc(c_first, 16)
            sp.dma_start(gates[:, 0:1], g_x[None, :].to_broadcast([P, 1])).then_inc(small_in, 16)
            sp.dma_start(gates[:, 1:2], g_f[None, :].to_broadcast([P, 1])).then_inc(small_in, 16)
            sp.dma_start(bg_sb[:, :], bg[None, :].to_broadcast([P, E])).then_inc(small_in, 16)
            sp.dma_start(wg_sb[:, :, :], Wg.rearrange("(k p) e -> p k e", p=P)).then_inc(small_in, 16)
            sp.dma_start(x_sb[:, 2], x_v[:, 2]).then_inc(x_first[2], 16)
            sp.dma_start(c_sb[:, 1], c_v[:, 1]).then_inc(c_in, 16)
            sp.dma_start(x_sb[:, 3], x_v[:, 3]).then_inc(x_in, 16)
            sp.dma_start(we_raw[:, 0:KC, :], we_v[:, 0:KC, :]).then_inc(w_first[0], 16)
            sp.dma_start(we_raw[:, KC:2 * KC, :], we_v[:, KC:2 * KC, :]).then_inc(w_first[1], 16)
            sp.dma_start(we_raw[:, 2 * KC:3 * KC, :], we_v[:, 2 * KC:3 * KC, :]).then_inc(w_in, 16)

            def store_x1(g):
                sp.wait_ge(x1_ready, TJ * g + TJ)
                sp.dma_start(out_v[:, ds(g, 1)], x_sb[:, ds(g % XR, 1)]).then_inc(x1_stored, 16)

            def store_h(g, first):
                sp.wait_ge(h_ready, TJ * g + TJ)
                if not first:
                    sp.wait_ge(h_stored, 16 * g)
                sp.dma_start(h_v[:, ds(g, 1)], h_sb[:, None]).then_inc(h_stored, 16)

            def load_x(g):
                sp.wait_ge(x1_stored, 16 * g + 16)
                sp.wait_ge(x_in, 16 * g + 16)
                sp.dma_start(x_sb[:, ds(g % XR, 1)], x_v[:, ds(g + XR, 1)]).then_inc(x_in, 16)

            def load_c(g, parity):
                sp.wait_ge(pv_done, TJ * g + TJ)
                sp.wait_ge(c_in, 16 * g + 16)
                sp.dma_start(c_sb[:, parity:parity + 1], c_v[:, ds(g + 2, 1)]).then_inc(c_in, 16)

            sp.dma_start(out[N:N + PADS, :], x.rearrange("b s d -> (b s) d")[0:PADS, :]).then_inc(pad_stored, 16)
            sp.dma_start(h_dram[N:N + PADS, :], x.rearrange("b s d -> (b s) d")[0:PADS, :]).then_inc(h_pad_stored, 16)
            sp.wait_ge(ids_filled, 2)
            sp.dma_start(ids_v, ids[:, 0]).then_inc(empty_stored, 16)

            def load_w(e):
                sp.wait_ge(w_in, 16 * (e - 2))
                sp.dma_start(we_raw[:, ds(KC * e, KC), :], we_v[:, ds(KC * e, KC), :]).then_inc(w_in, 16)

            def group(g, parity, first):
                load_w(g + 3)
                store_x1(g)
                load_c(g, parity)
                store_h(g, first)
                load_x(g)

            group(0, 0, True)
            group(1, 1, False)
            with sp.Fori(1, GROUPS // 2 - 2) as i:
                for parity in range(2):
                    group(2 * i + parity, parity, False)
            for g in range(GROUPS - XR, GROUPS):
                if g + 3 < E:
                    load_w(g + 3)
                sp.wait_ge(x1_stored, 16 * g)
                store_x1(g)
                if g + 2 < GROUPS:
                    load_c(g, g % 2)
                store_h(g, False)
                if g == AHEAD:
                    sp.wait_ge(ids_stored, 16 * TJ * TOPK * AHEAD)
                    sp.dma_start(ids[:, 0], ids_v).then_inc(ids_in, 16)
                    sp.wait_ge(g_done, KC * GROUPS)
                    sp.wait_ge(row_in[1], 16)
                    sp.dma_start(be_sb[:, :, :], be[None, :, :].to_broadcast([P, E, D])).then_inc(be_in, 16)

            def clear(b, u):
                later = not isinstance(b, int)
                need = [16 if not later and b - d < BU else
                        sp.value_load(added_need[0:1, d - 1, ds(b, 1)], min_val=16, max_val=16 * BLOCKS)
                        for d in range(1, BU)]
                for d in range(BU - 1, 0, -1):
                    sp.wait_ge(added[(u - d) % BU], need[d - 1])
                sp.sem_inc(rows_free, 1)

            sp.wait_ge(others_known, 1)
            for b in range(BU, 2 * BU):
                clear(b, b % BU)
            sp.wait_ge(others_known, 2)
            with sp.Fori(2, TURNS) as i:
                for u in range(BU):
                    clear(i * BU + u, u)
            for b in range(TURNS * BU, BLOCKS):
                clear(b, b % BU)
            sp.wait_ge(pad_stored, 16)
            sp.wait_ge(h_pad_stored, 16)
            for u in range(BU):
                sp.wait_ge(added[u], 16 * ((BLOCKS - 1 - u) // BU + 1))

        @block.scalar
        def _(act):
            def piece_hi(e, k):
                if isinstance(e, int) and e < 2:
                    act.wait_ge(w_first[e], 16)
                elif k == 0:
                    act.wait_ge(w_in, 16 * (e - 1))
                nc.scalar.copy(we_hi[:, ds(KC * e + k, 1), :], we_raw[:, ds(KC * e + k, 1), :]).then_inc(w_hi_done, 1)

            act.wait_ge(small_in, 64)
            nc.scalar.activation(tanh_g[:, :], gates[:, :], ACT.Tanh).then_inc(tanh_done, 1)

            def norm1(g):
                act.wait_ge(rstd1_done, 2 * g + 2)
                if not (isinstance(g, int) and g == 0):
                    act.wait_ge(row_summed, TJ * g)
                for j in range(TJ):
                    nc.scalar.activation(a_sb[:, j], x_sb[:, ds(g % XR, 1), j], ACT.Identity, bias=shift1[:, j:j + 1],
                                         scale=rstd1[:, j:j + 1]).then_inc(a_ready, 1)

            norm1(0)
            for c in range(KC):
                act.wait_ge(m_done, c + 1)
                nc.scalar.copy(m_hi[:, c], m_ps[c][:, :]).then_inc(m_hi_done, 1)

            def evac_a(g, j):
                act.wait_ge(aT_done, TJ * g + j + 1)
                nc.scalar.copy(aT_hi[:, :, j * P:(j + 1) * P], tpv[a_tp[j]]).then_inc(aT_hi_done, 1)

            def evac_g(g, c):
                act.wait_ge(g_done, KC * g + c + 1)
                nc.scalar.activation(gT[:, c], gb[c % 2][:, 0:GT], ACT.Identity,
                                     bias=w_vec[:, c:c + 1]).then_inc(g_evac, 1)

            for j in range(TJ):
                evac_a(0, j)
            for k in range(KC):
                piece_hi(0, k)
            norm1(1)
            act.wait_ge(vec_evac, 1)

            def evac_c(g, j):
                act.wait_ge(cT_done, TJ * g + j + 1)
                nc.scalar.copy(cT[:, j], tpv[c_tp[j]]).then_inc(cT_evac, 1)

            def evac_p(g):
                for j in range(TJ):
                    act.wait_ge(pt_done, TJ * g + j + 1)
                    nc.scalar.copy(p_sb[:, j], sc[j][:, P:2 * P]).then_inc(pt_evac, 1)

            def exps(g):
                for j in range(TJ):
                    act.wait_ge(neg_done, TJ * g + j + 1)
                    for r0 in (0, S):
                        rr = slice(r0, r0 + S)
                        e = nc.scalar.activation(p_sb[rr, j, r0:r0 + S], s_sb[rr, j], ACT.Exp,
                                                 bias=neg_peak[rr, j:j + 1], scale=SCALE,
                                                 accum_out=exp_sum[rr, j:j + 1])
                    e.then_inc(exp_done, 1)

            def group(g, first, ahead):
                evac_g(g + 1, 0)
                exps(g)
                evac_g(g + 1, 1)
                if ahead:
                    piece_hi(g + 2, 0)
                evac_g(g + 1, 2)
                if not first:
                    evac_h(g - 1, former_hv)
                if ahead:
                    piece_hi(g + 2, 1)
                evac_g(g + 1, 3)
                if ahead:
                    norm1(g + 2)
                evac_p(g)
                if ahead:
                    piece_hi(g + 2, 2)
                    for j in range(TJ):
                        evac_a(g + 2, j)
                evac_c(g + 1, 0)
                evac_c(g + 1, 1)
                if ahead:
                    piece_hi(g + 2, 3)

            def evac_h(g, banks):
                for j in range(TJ):
                    act.wait_ge(hT_done, TJ * g + j + 1)
                    nc.scalar.copy(hT[:, j], banks[j]).then_inc(hT_evac, 1)

            evac_g(0, 0)
            evac_g(0, 1)
            piece_hi(1, 0)
            evac_g(0, 2)
            for j in range(TJ):
                evac_c(0, j)
            evac_g(0, 3)
            for j in range(TJ):
                evac_a(1, j)
            for k in range(1, KC):
                piece_hi(1, k)
            group(0, True, True)
            with act.Fori(1, GROUPS - 2) as g:
                group(g, False, True)
            group(GROUPS - 2, False, False)

            def block_hi(b, u):
                act.wait_ge(xT_done, b + 1)
                nc.scalar.copy(xT_hi[:, u % XU], tbv[u % XU]).then_inc(xT_hi_done, 1)

            def pick(b, u, at, known):
                c = act.value_load(column_of[0:1, ds(b, 1)], min_val=0, max_val=2 * COLS - 1)
                nc.scalar.copy(at[:, u:u + 1], flat_ids[:, ds(c, 1)]).then_inc(known, 1)

            def pick_next(b, u):
                pick(b + BU, u, gather_at, gather_known)

            def pick_add(b, u, count):
                if count is not None:
                    act.wait_ge(added[u], 16 * count)
                pick(b, u, add_at, add_known)

            act.wait_ge(lists_known, 2)
            act.wait_ge(ids_in, 16)
            block_hi(0, 0)
            exps(GROUPS - 1)
            evac_h(GROUPS - 2, former_hv)
            block_hi(1, 1)
            evac_p(GROUPS - 1)
            pick_add(0, 0, None)
            for b in range(2, 2 * BU):
                if b == BU:
                    evac_h(GROUPS - 1, last_hv)
                block_hi(b, b % BU)
                pick_add(b - 1, (b - 1) % BU, 1 if b > BU else None)
            for b in range(2 * BU, EARLY):
                block_hi(b, b % BU)
                if b == 2 * BU + 1:
                    act.wait_ge(lists_known, 4)
                    act.wait_ge(ids_stored, 16 * TJ * TOPK * GROUPS)
                    act.dma_start(ids[:, 1], ids_v).then_inc(ids_in, 16)
                    act.wait_ge(ids_in, 32)
                    pick_next(b - 1, (b - 1) % BU)
                if b > 2 * BU:
                    pick_next(b, b % BU)
                pick_add(b - 1, (b - 1) % BU, (b - 1) // BU)
            with act.Fori(EARLY // BU, TURNS - 1) as i:
                for u in range(BU):
                    block_hi(i * BU + u, u)
                    pick_next(i * BU + u, u)
                    pick_add(i * BU + u - 1, (u - 1) % BU, i - (u == 0))
            for b in range((TURNS - 1) * BU, BLOCKS):
                block_hi(b, b % BU)
                if b + BU < BLOCKS:
                    pick_next(b, b % BU)
                pick_add(b - 1, (b - 1) % BU, (b - 1) // BU)
            pick_add(BLOCKS - 1, (BLOCKS - 1) % BU, (BLOCKS - 1) // BU)

        @block.vector
        def _(dve):
            nc.vector.memset(half_neg[:, :], -0.5).then_inc(filled, 1)
            nc.vector.memset(ident[:, :], 1.0).then_inc(filled, 1)
            nc.vector.memset(ones_b[:, :], 1.0).then_inc(filled, 1)
            nc.vector.memset(earlier[:, :], 1.0).then_inc(filled, 1)
            nc.vector.memset(p_sb[:, :, :], 0.0)
            nc.vector.memset(ones8[:, :], 1.0)
            nc.vector.memset(early[:, :], 0.0)
            nc.vector.memset(taken[:, :], 0.0).then_inc(mask_step, 1)

            def stats1_tile(g, j):
                nc.vector.bn_stats(st1[:, j], x_sb[:, ds(g % XR, 1), j]).then_inc(st1_step, 1)

            def stats1_end(q):
                for j in range(TJ):
                    nc.vector.bn_aggr(mv1[:, j], st1[:, j]).then_inc(st1_step, 1)
                dve.wait_ge(st1_step, 5 * q + 4)
                nc.vector.tensor_scalar(neg_mean1[:, :], mv1[:, :, 0], -1.0, None, ALU.mult)
                nc.vector.tensor_scalar(ve1[:, :], mv1[:, :, 1], EPS, None, ALU.add).then_inc(st1_step, 1)

            def stats1(q, g):
                for j in range(TJ):
                    stats1_tile(g, j)
                dve.drain()
                stats1_end(q)

            def lo_a(g, j):
                dve.wait_ge(aT_hi_done, TJ * g + j + 1)
                t = slice(j * P, (j + 1) * P)
                nc.vector.tensor_tensor(aT_lo[:, :, t], tpv[a_tp[j]], aT_hi[:, :, t].bitcast(fp32),
                                        ALU.subtract).then_inc(aT_lo_done, 1)

            def row_products(g):
                for j in range(TJ):
                    nc.vector.scalar_tensor_tensor(a_sb[:, j], a_sb[:, j], 1.0, u_rows[:, :], ALU.mult, ALU.mult,
                                                   accum_out=row_sum[:, j:j + 1]).then_inc(row_summed, 1)

            def row_sums(g):
                dve.wait_ge(row_summed, TJ * g + TJ)
                nc.vector.tensor_scalar(row_term[:, :], row_sum[:, :], bb[:, 0:1], None, ALU.add).then_inc(terms_done, 1)

            def read_ranks(g):
                dve.wait_ge(ranks_done, g + 1)
                nc.vector.tensor_tensor(slot_prod[:, :, :, :], chosen[:, :, :, :],
                                        rk_ps[:, :, None, :].to_broadcast([P, TJ, TOPK, E]),
                                        ALU.mult)
                nc.vector.tensor_scalar(place0[:, :, :], best_f[:, :, :], float(CPE * P), None,
                                        ALU.mult).then_inc(ranks_read, 1)

            def slots_rank(g):
                dve.wait_ge(ranks_read, g + 1)
                nc.vector.tensor_reduce(rank_of[:, :, :], slot_prod[:, :, :, :], AX.X, ALU.add).then_inc(slot_step, 1)

            def slots_place(g):
                dve.wait_ge(slot_step, SS * g + 1)
                nc.vector.tensor_tensor(place[:, :, :], place0[:, :, :], rank_of[:, :, :],
                                        ALU.add).then_inc(slot_step, 1)

            def slots_whole(g):
                dve.wait_ge(slot_step, SS * g + 2)
                nc.vector.tensor_copy(place_i[:, :, :], place[:, :, :]).then_inc(slot_step, 1)

            def slots_modulo(g):
                dve.wait_ge(slot_step, SS * g + 3)
                nc.vector.tensor_scalar(slot_i[:, :, :], place_i[:, :, :], P - 1, None,
                                        ALU.bitwise_and).then_inc(slot_step, 1)
                nc.vector.tensor_scalar(place[:, :, :], place[:, :, :], 1.0 / P, None, ALU.mult)

            def slots_float(g):
                dve.wait_ge(slot_step, SS * g + 4)
                nc.vector.tensor_copy(slot_f[:, :, :], slot_i[:, :, :]).then_inc(slot_step, 1)

            def slots_id(g, first):
                dve.wait_ge(slot_step, SS * g + 5)
                last_early = isinstance(g, int) and g == AHEAD - 1
                if not first and not last_early:
                    dve.wait_ge(ids_stored, 16 * TJ * TOPK * g)
                to = early_id_at if last_early else id_at
                nc.vector.scalar_tensor_tensor(to[:, :].rearrange("p (j c) -> p j c", c=TOPK), slot_f[:, :, :],
                                               COLS - 1.0 / P, place[:, :, :], ALU.mult, ALU.add).then_inc(id_known, 1)

            def slots(g, first):
                slots_rank(g)
                slots_place(g)
                slots_whole(g)
                slots_modulo(g)
                slots_float(g)
                slots_id(g, first)

            dve.wait_ge(x_first[0], 16)
            stats1(0, 0)
            dve.wait_ge(bias_in, 32)
            nc.vector.tensor_copy(bk_rows[:, :, :], bqk[:, 1, :, None].to_broadcast([P, KC, P])).then_inc(bk_spread, 1)
            for c in range(KC):
                dve.wait_ge(m_hi_done, c + 1)
                nc.vector.tensor_tensor(m_lo[:, c], m_ps[c][:, :], m_hi[:, c].bitcast(fp32),
                                        ALU.subtract).then_inc(m_lo_done, 1)
            dve.wait_ge(x_first[1], 16)
            stats1(1, 1)
            dve.wait_ge(u_done, 1)
            nc.vector.tensor_copy(u_rows[:, :], u_ps[:, :])
            for j in range(TJ):
                lo_a(0, j)
            dve.wait_ge(vec_done, 1)
            nc.vector.tensor_copy(bb[:, :], bb_ps)
            nc.vector.tensor_copy(w_vec[:, :], w_ps).then_inc(vec_evac, 1)
            dve.wait_ge(vec_evac, 1)
            dve.wait_ge(a_ready, TJ)
            row_products(0)
            row_sums(0)
            dve.wait_ge(tanh_done, 1)
            nc.vector.tensor_scalar(ffn_gain[:, :], tanh_g[:, 1:2], 1.0 / TOPK, None, ALU.mult).then_inc(gain_done, 1)
            for j in range(TJ):
                lo_a(1, j)

            def soft(g, j):
                dve.wait_ge(scores_done, TJ * g + j + 1)
                if j == 0:
                    dve.wait_ge(terms_done, g + 1)
                for r0 in (0, S):
                    rr = slice(r0, r0 + S)
                    nc.vector.tensor_scalar(s_sb[rr, j], sc[j][rr, r0:r0 + S], row_term[rr, j:j + 1], None,
                                            ALU.add, ALU.max, accum_out=peak[rr, j:j + 1]).then_inc(peak_done, 1)
                dve.wait_ge(peak_done, 2 * (TJ * g + j + 1))
                nc.vector.tensor_scalar(neg_peak[:, j:j + 1], peak[:, j:j + 1], -SCALE, None,
                                        ALU.mult).then_inc(neg_done, 1)

            def masks_logit(g):
                dve.wait_ge(logits_done, g + 1)
                nc.vector.tensor_tensor(logit[:, :, :], l_ps, bg_sb[:, None, :].to_broadcast([P, TJ, E]),
                                        ALU.add).then_inc(logits_read, 1)

            def masks_max(g):
                dve.drain()
                for j in range(TJ):
                    nc.vector.max(best[:, j], logit[:, j]).then_inc(mask_step, 1)

            def masks_index(g):
                dve.drain()
                for j in range(TJ):
                    nc.vector.max_index(best_at[:, j], best[:, j], logit[:, j]).then_inc(mask_step, 1)

            def masks_float(g):
                dve.wait_ge(mask_step, MS * g + 5)
                nc.vector.tensor_copy(best_f[:, :, :], best_at[:, :, 0:TOPK]).then_inc(mask_step, 1)

            def masks_hot(g):
                dve.wait_ge(mask_step, MS * g + 6)
                nc.vector.tensor_tensor(chosen[:, :, :, :], iota_e[:, None, None, :].to_broadcast([P, TJ, TOPK, E]),
                                        best_f[:, :, :, None].to_broadcast([P, TJ, TOPK, E]),
                                        ALU.is_equal).then_inc(mask_step, 1)

            def masks_sum(g):
                dve.wait_ge(mask_step, MS * g + 7)
                nc.vector.tensor_tensor(mask[:, :, :], chosen[:, :, 0], chosen[:, :, 1], ALU.add).then_inc(mask_ready, 1)

            def masks(g):
                masks_logit(g)
                masks_max(g)
                masks_index(g)
                masks_float(g)
                masks_hot(g)
                masks_sum(g)

            def taken_first(g):
                nc.vector.tensor_tensor(taken[:, :], taken[:, :], mask[:, 0], ALU.add).then_inc(mask_step, 1)

            def taken_second(g):
                dve.wait_ge(mask_step, MS * g + 8)
                nc.vector.tensor_tensor(taken[:, :], taken[:, :], mask[:, 1], ALU.add).then_inc(mask_step, 1)

            def taken_more(g):
                taken_first(g)
                taken_second(g)

            def norm2(g, first):
                dve.wait_ge(rstd2_done, g + 1)
                if not first:
                    dve.wait_ge(hT_done, TJ * g)
                    dve.wait_ge(h_stored, 16 * g)
                for j in range(TJ):
                    nc.vector.tensor_scalar(h_sb[:, j], x_sb[:, ds(g % XR, 1), j], mv2[:, j, 0:1],
                                            rstd2[:, j:j + 1], ALU.subtract, ALU.mult).then_inc(h_ready, 1)

            def after(n):
                dve.wait_ge(route_step, n)

            def lists(part):
                r0, b0, b1, late = (0, 0, EARLY, 0) if part == 0 else (14, EARLY, BLOCKS, 1)
                nb = b1 - b0
                b_shape = [1, nb, E]
                dve.wait_ge(count_done, part + 1)
                nc.vector.tensor_scalar(count_i[:, :], cnt_ps, float((P - 1) * late), None,
                                        ALU.add).then_inc(route_step, 1)
                after(r0 + 1)
                nc.vector.tensor_scalar(nblk_i[:, :], count_i[:, :], P.bit_length() - 1, None,
                                        ALU.arith_shift_right).then_inc(route_step, 1)
                after(r0 + 2)
                nc.vector.tensor_copy(nblk[:, :], nblk_i[:, :]).then_inc(route_step, 1)
                after(r0 + 3)
                if late:
                    nc.vector.tensor_tensor(nblk[:, :], nblk[:, :], early[:, 0:E], ALU.subtract).then_inc(route_step, 1)
                    after(r0 + 4)
                r1 = r0 + 3 + late
                nc.vector.tensor_tensor_scan(blk_end[:, :], ones8[0:1, :], nblk[:, :], 0.0, ALU.mult,
                                             ALU.add).then_inc(route_step, 1)
                nc.vector.tensor_scalar(stride[:, :], nblk[:, :], -1.0, float(CPE), ALU.mult,
                                        ALU.add).then_inc(route_step, 1)
                after(r1 + 2)
                if late:
                    nc.vector.tensor_tensor(stride2[:, :], stride[:, :], early[:, 1:E + 1],
                                            ALU.add).then_inc(route_step, 1)
                    after(r1 + 3)
                    nc.vector.tensor_tensor(stride[:, :], stride2[:, :], early[:, 0:E],
                                            ALU.subtract).then_inc(route_step, 1)
                r2 = r1 + 2 + 2 * late
                nc.vector.tensor_tensor(past[:, 0:nb, :], iota_b[:, 0:nb, None].to_broadcast(b_shape),
                                        blk_end[:, None, :].to_broadcast(b_shape), ALU.is_ge).then_inc(route_step, 1)
                after(r2 + 1)
                nc.vector.tensor_tensor(skip[:, 0:nb, :], past[:, 0:nb, :], stride[:, None, :].to_broadcast(b_shape),
                                        ALU.mult).then_inc(route_step, 1)
                nc.vector.tensor_reduce(n_past[:, b0:b1], past[:, 0:nb, :], AX.X, ALU.add).then_inc(route_step, 1)
                after(r2 + 3)
                nc.vector.tensor_scalar(expert_of[:, b0:b1], n_past[:, b0:b1], float(E - 1), None,
                                        ALU.min).then_inc(lists_known, 1)
                nc.vector.tensor_reduce(skipped[:, 0:nb], skip[:, 0:nb, :], AX.X, ALU.add).then_inc(route_step, 1)
                nc.vector.tensor_scalar(column0[:, 0:nb], iota_b[:, 0:nb], early[:, 0:1], float(COLS * part),
                                        ALU.add, ALU.add).then_inc(route_step, 1)
                after(r2 + 5)
                nc.vector.tensor_tensor(column_of[:, b0:b1], column0[:, 0:nb], skipped[:, 0:nb],
                                        ALU.add).then_inc(lists_known, 1)

            def others(b0, b1):
                for d in range(1, BU):
                    nc.vector.tensor_tensor(other[:, d - 1, b0:b1], expert_of[:, b0:b1],
                                            expert_of[:, b0 - d:b1 - d], ALU.not_equal).then_inc(other_done, 1)
                dve.wait_ge(other_done, (BU - 1) * (1 + (b0 == EARLY)))
                dve.wait_ge(const_done, CONSTS)
                nc.vector.scalar_tensor_tensor(added_need[:, :, b0:b1], other[:, :, b0:b1], 16.0,
                                               added_base[:, :, b0:b1], ALU.mult, ALU.add).then_inc(others_known, 1)

            def early_blocks():
                r2 = 12
                nc.vector.tensor_tensor(blk_first[:, :], blk_end[:, :], nblk[:, :], ALU.subtract).then_inc(route_step, 1)
                nc.vector.tensor_scalar(early_end[:, :], blk_end[:, :], float(EARLY), None,
                                        ALU.min).then_inc(route_step, 1)
                after(r2)
                nc.vector.tensor_scalar(early_first[:, :], blk_first[:, :], float(EARLY), None,
                                        ALU.min).then_inc(route_step, 1)
                after(r2 + 1)
                nc.vector.tensor_tensor(early[:, 0:E], early_end[:, :], early_first[:, :],
                                        ALU.subtract).then_inc(route_step, 1)

            def att_gains(g):
                dve.wait_ge(inv_done, g + 1)
                nc.vector.tensor_scalar(att_gain[:, :], exp_inv[:, :], tanh_g[:, 0:1], None,
                                        ALU.mult).then_inc(att_gain_done, 1)

            def inverses(g):
                dve.wait_ge(exp_done, TJ * g + TJ)
                nc.vector.reciprocal(exp_inv[:, :], exp_sum[:, :]).then_inc(inv_done, 1)

            def x1_tile(g, j):
                if j == 0:
                    dve.wait_ge(att_gain_done, g + 1)
                dve.wait_ge(pv_done, TJ * g + j + 1)
                nc.vector.scalar_tensor_tensor(x_sb[:, ds(g % XR, 1), j], sc[j][:, :], att_gain[:, j:j + 1],
                                               x_sb[:, ds(g % XR, 1), j], ALU.mult, ALU.add).then_inc(x1_ready, 1)

            def stats2(g):
                dve.drain()
                for j in range(TJ):
                    nc.vector.bn_stats(st2[:, j], x_sb[:, ds(g % XR, 1), j]).then_inc(st2_step, 1)
                dve.drain()
                for j in range(TJ):
                    nc.vector.bn_aggr(mv2[:, j], st2[:, j]).then_inc(st2_step, 1)
                dve.wait_ge(st2_step, 5 * g + 4)
                nc.vector.tensor_scalar(ve2[:, :], mv2[:, :, 1], EPS, None, ALU.add).then_inc(st2_step, 1)

            def group(g, first, ahead, ranked=True):
                if isinstance(g, int) and g == AHEAD + 1:
                    slots(g - 2, False)
                for j in range(TJ):
                    soft(g, j)
                if not first:
                    norm2(g - 1, isinstance(g, int) and g == 1)
                if isinstance(g, int) and g == AHEAD + 1:
                    lists(0)
                if ahead:
                    if first:
                        dve.wait_ge(x_first[2], 16)
                    else:
                        dve.wait_ge(x_in, 16 * g)
                    stats1(g + 2, g + 2)
                dve.wait_ge(a_ready, TJ * (g + 2))
                row_products(g + 1)
                row_sums(g + 1)
                inverses(g)
                if ranked:
                    slots_rank(g - 2)
                    slots_place(g - 2)
                    slots_whole(g - 2)
                    slots_modulo(g - 2)
                if not first:
                    masks_logit(g - 1)
                att_gains(g)
                if not first:
                    masks_max(g - 1)
                if ranked:
                    slots_float(g - 2)
                if not first:
                    masks_index(g - 1)
                if ranked:
                    slots_id(g - 2, isinstance(g, int) and g == 2)
                if not first:
                    masks_float(g - 1)
                    masks_hot(g - 1)
                    masks_sum(g - 1)
                if ahead:
                    for j in range(TJ):
                        lo_a(g + 2, j)
                if not first:
                    read_ranks(g - 1)
                    taken_first(g - 1)
                x1_tile(g, 0)
                if not first:
                    taken_second(g - 1)
                x1_tile(g, 1)
                stats2(g)

            group(0, True, True, ranked=False)
            group(1, False, True, ranked=False)
            group(2, False, True)
            with dve.Fori(3, GROUPS - 2) as g:
                group(g, False, True)
            group(GROUPS - 2, False, False, ranked=False)

            dve.wait_ge(gain_done, 1)

            def block_lo(b, u):
                dve.wait_ge(xT_hi_done, b + 1)
                nc.vector.tensor_tensor(xT_lo[:, u % XU], tbv[u % XU], xT_hi[:, u % XU].bitcast(fp32),
                                        ALU.subtract).then_inc(xT_lo_done, 1)

            def block_expert(b):
                return dve.value_load(expert_of[0:1, ds(b, 1)], min_val=0, max_val=E - 1)

            def block_y(b, u, e, first, done=None):
                dve.wait_ge(y_done, b + 1)
                nc.vector.tensor_tensor(y_raw[:, u], yb_of(b, u)[:, :], be_sb[:, ds(e, 1), :], ALU.add).then_inc(y_biased, 1)
                if not first:
                    dve.wait_ge(added[u], done)
                dve.wait_ge(y_biased, b + 1)
                nc.vector.tensor_scalar(y_sb[:, u], y_raw[:, u], 0.0, ffn_gain[:, 0:1], ALU.max,
                                        ALU.mult).then_inc(y_ready, 1)

            def lo(b):
                block_lo(b, b % BU)

            def y(b, e=None):
                if e is None:
                    e = block_expert(b)
                block_y(b, b % BU, e, b < BU, 16 * (b // BU))

            g = GROUPS - 1
            for j in range(TJ):
                soft(g, j)
            lo(0)
            norm2(g - 1, False)
            inverses(g)
            slots(g - 2, False)
            att_gains(g)
            lo(1)
            dve.wait_ge(lists_known, 2)
            e0 = block_expert(0)
            masks(g - 1)
            for j in range(TJ):
                x1_tile(g, j)
            stats2(g)
            dve.wait_ge(be_in, 16)
            dve.wait_ge(x1_stored, 16 * (GROUPS - 2))
            y(0, e0)
            lo(2)
            read_ranks(g - 1)
            taken_more(g - 1)
            norm2(g, False)
            lo(3)
            y(1)
            e2 = block_expert(2)
            slots(g - 1, False)
            y(2, e2)
            lo(4)
            early_blocks()
            others(BU, EARLY)
            y(3)
            masks(g)
            lo(5)
            y(4)
            read_ranks(g)
            taken_more(g)
            slots(g, False)
            lo(6)
            y(5)
            lo(7)
            e6 = block_expert(6)
            lists(1)
            lo(8)
            y(6, e6)
            y(7)
            others(EARLY, BLOCKS)
            with dve.Fori(2, TURNS) as i:
                for u in range(BU):
                    block_lo(i * BU + u + 1, (u + 1) % BU)
                    block_y(i * BU + u, u, block_expert(i * BU + u), False, 16 * i)
            for b in range(TURNS * BU, BLOCKS):
                if b + 1 < BLOCKS:
                    block_lo(b + 1, (b + 1) % BU)
                block_y(b, b % BU, block_expert(b), False, 16 * (b // BU))

        @block.gpsimd
        def _(pool):
            def piece_lo(e, k):
                n = KC * e + k
                pool.wait_ge(w_hi_done, n + 1)
                nc.gpsimd.tensor_tensor(we_lo[:, ds(n, 1), :], we_raw[:, ds(n, 1), :],
                                        we_hi[:, ds(n, 1), :].bitcast(fp32), ALU.subtract).then_inc(w_lo_done, 1)

            def rstd(q, steps, var_eps, rstd_, done):
                pool.wait_ge(steps, 5 * q + 5)
                nc.gpsimd.tensor_tensor(rstd_[:, :], var_eps[:, :], half_neg[:, :], ALU.pow).then_inc(done, 1)

            def rstd1_of(q):
                rstd(q, st1_step, ve1, rstd1, rstd1_done)
                pool.wait_ge(rstd1_done, 2 * q + 1)
                nc.gpsimd.tensor_tensor(shift1[:, :], neg_mean1[:, :], rstd1[:, :], ALU.mult).then_inc(rstd1_done, 1)

            nc.gpsimd.memset(gate[:, :], 0.0)
            pool.wait_ge(filled, 4)
            nc.gpsimd.affine_select(ident[:, :], ident[:, :], [[1, P]], ALU.is_equal, 0.0, base=0,
                                    channel_multiplier=-1).then_inc(ident_done, 1)
            nc.gpsimd.affine_select(earlier[:, :], earlier[:, :], [[1, P]], ALU.is_gt, 0.0, base=0,
                                    channel_multiplier=-1).then_inc(const_done, 1)
            rstd1_of(0)
            nc.gpsimd.iota(iota_e[:, :], [[1, E]], base=0, channel_multiplier=0,
                           allow_small_or_imprecise_dtypes=True).then_inc(const_done, 1)
            nc.gpsimd.iota(iota_b[:, :], [[1, BLOCKS]], base=0, channel_multiplier=0,
                           allow_small_or_imprecise_dtypes=True).then_inc(const_done, 1)
            for d in range(1, BU):
                nc.gpsimd.iota(added_base[:, d - 1, d:d + BU * (BLOCKS // BU + 1)], [[16, BLOCKS // BU + 1], [0, BU]], base=0,
                               channel_multiplier=0, allow_small_or_imprecise_dtypes=True).then_inc(const_done, 1)
            nc.gpsimd.iota(token[:, :], [[P, TILES]], base=0, channel_multiplier=1).then_inc(const_done, 1)
            nc.gpsimd.iota(ids[:, 0, 0:E * CPE], [[0, E * CPE]], base=N, channel_multiplier=1).then_inc(ids_filled, 1)
            nc.gpsimd.iota(ids[:, 0, E * CPE:COLS], [[0, CPE // BU], [P, BU]], base=N + P,
                           channel_multiplier=1).then_inc(ids_filled, 1)
            rstd1_of(1)

            def store_ids(g, first):
                last_early = isinstance(g, int) and g == AHEAD - 1
                at, numbers = (early_id_at, early_token_at) if last_early else (id_at, token_at)
                pool.wait_ge(id_known, g + 1)
                if first:
                    pool.wait_ge(empty_stored, 16)
                    pool.wait_ge(const_done, CONSTS)
                else:
                    if not last_early:
                        pool.wait_ge(ids_stored, 16 * TJ * TOPK * g)
                nc.gpsimd.tensor_copy(numbers[:, :], token[:, ds(TJ * g, TJ)]).then_inc(token_copied, 1)
                pool.wait_ge(token_copied, g + 1)
                nc.gpsimd.tensor_tensor(gate[:, 0:1], gate[:, 0:1], gate[:, 0:1], ALU.add)
                for n in range(TJ * TOPK):
                    pool.indirect_dma_start(out=ids_dram, out_offset=bass.IndirectOffsetOnAxis(ap=at[:, n:n + 1], axis=0),
                                            in_=numbers[:, n // TOPK:n // TOPK + 1], in_offset=None).then_inc(ids_stored, 16)

            def pieces(e, ks):
                for k in ks:
                    piece_lo(e, k)

            def group(g, ranked, first=False, last=False):
                rstd1_of(g + 2)
                pieces(g + 2, (0, 1, 2))
                if ranked:
                    store_ids(g - 2, first)
                rstd(g, st2_step, ve2, rstd2, rstd2_done)
                if not last:
                    pieces(g + 2, (3,))

            for e in range(2):
                pieces(e, range(KC))
            group(0, False)
            group(1, False)
            group(2, True, first=True)
            with pool.Fori(3, GROUPS - 3) as g:
                group(g, True)
            group(GROUPS - 3, True, last=True)
            store_ids(GROUPS - 4, False)
            pieces(GROUPS - 1, (3,))

            def gather(b, u):
                known = h_dram[0:AHEAD * GT, :] if isinstance(b, int) and b < EARLY else h_dram
                pool.indirect_dma_start(out=rows[:, u, :], out_offset=None, in_=known,
                                        in_offset=bass.IndirectOffsetOnAxis(ap=gather_at[:, u:u + 1], axis=0)
                                        ).then_inc(row_in[u], 16)

            def add(b, u):
                into = out[0:AHEAD * GT, :] if isinstance(b, int) and b < EARLY else out
                pool.indirect_dma_start(out=into, out_offset=bass.IndirectOffsetOnAxis(ap=add_at[:, u:u + 1], axis=0),
                                        in_=y_sb[:, u, :], in_offset=None, compute_op=ALU.add).then_inc(added[u], 16)

            def pick(b, u):
                c = pool.value_load(column_of[0:1, ds(b, 1)], min_val=0, max_val=2 * COLS - 1)
                nc.gpsimd.tensor_copy(gather_at[:, u:u + 1], flat_ids[:, ds(c, 1)]).then_inc(first_known, 1)

            def turn(b, u, more):
                v = (u + 2) % BU
                if not (isinstance(b, int) and b == 0):
                    pool.wait_ge(gated, b)
                if more:
                    pool.wait_ge(gather_known, b + BU + 3 - EARLY)
                pool.wait_ge(add_known, b + 1)
                pool.wait_ge(y_ready, b + 1)
                if isinstance(b, int) and b < BU:
                    if b:
                        pool.wait_ge(added[(b - 1) % BU], 16 * ((b - 1) // BU + 1))
                else:
                    pool.wait_ge(rows_free, b - BU + 1)
                nc.gpsimd.tensor_tensor(gate[:, 1:2], gate[:, 1:2], gate[:, 1:2], ALU.add).then_inc(gated, 1)
                add(b, u)
                if more:
                    gather(b + BU + 2, v)

            pool.wait_ge(lists_known, 2)
            pool.wait_ge(ids_in, 16)
            pool.wait_ge(h_stored, 16 * AHEAD)
            pool.wait_ge(g_done, KC * GROUPS)
            for u in range(BU):
                pick(u, u)
                pool.wait_ge(first_known, u + 1)
                gather(u, u)
                if u == 1:
                    rstd(GROUPS - 2, st2_step, ve2, rstd2, rstd2_done)

            def gather_next(b):
                pool.wait_ge(xT_done, b - BU + 1)
                pick(b, b % BU)
                pool.wait_ge(first_known, b + 1)
                gather(b, b % BU)

            gather_next(BU)
            store_ids(GROUPS - 3, False)
            pool.wait_ge(x1_stored, 16 * AHEAD)
            rstd(GROUPS - 1, st2_step, ve2, rstd2, rstd2_done)
            turn(0, 0, False)
            gather_next(BU + 1)
            gather_next(BU + 2)
            turn(1, 1, False)
            gather_next(BU + 3)
            store_ids(GROUPS - 2, False)
            for b in range(2, EARLY - BU - 2):
                turn(b, b % BU, False)
                gather_next(b + BU + 2)
                if b == 3:
                    store_ids(GROUPS - 1, False)
            pool.wait_ge(lists_known, 4)
            pool.wait_ge(ids_in, 32)
            pool.wait_ge(h_stored, 16 * GROUPS)
            pool.wait_ge(h_pad_stored, 16)
            pool.wait_ge(x1_stored, 16 * GROUPS)
            pool.wait_ge(pad_stored, 16)
            pool.wait_ge(gather_known, 1)
            gather(EARLY, 0)
            turn(EARLY - BU - 2, (EARLY - BU - 2) % BU, False)
            for b in range(EARLY - BU - 1, 2 * BU):
                turn(b, b % BU, True)
            with pool.Fori(2, TURNS - 1) as i:
                for u in range(BU):
                    turn(i * BU + u, u, True)
            for b in range((TURNS - 1) * BU, BLOCKS):
                turn(b, b % BU, b + BU + 2 < BLOCKS)
            for u in range(BU):
                pool.wait_ge(added[u], 16 * ((BLOCKS - 1 - u) // BU + 1))

        @block.tensor
        def _(pe):
            def chunks4(dst, src, done):
                for k in range(KC):
                    t = nc.tensor.transpose(dst[:, k * P:(k + 1) * P], src(k), ident[:, :])
                t.then_inc(done, 1)

            def product3(dst, k3, k_hi, k_lo, rhs_hi, rhs_lo):
                for k in range(k3):
                    nc.tensor.matmul(dst, k_hi(k), rhs_hi(k), start=(k == 0), stop=False)
                    nc.tensor.matmul(dst, k_hi(k), rhs_lo(k), start=False, stop=False)
                    last = nc.tensor.matmul(dst, k_lo(k), rhs_hi(k), start=False, stop=(k == k3 - 1))
                return last

            for k in range(KC):
                pe.wait_ge(proj_in[k], 32)
                for c in range(KC):
                    m = nc.tensor.matmul(m_ps[c][:, :], wq_sb[:, k, c * P:(c + 1) * P], wk_sb[:, k, :],
                                         start=(k == 0), stop=(k == KC - 1))
                    if k == KC - 1:
                        m.then_inc(m_done, 1)
            pe.wait_ge(bk_spread, 1)
            for k in range(KC):
                m = nc.tensor.matmul(u_ps[:, :], bk_rows[:, k, :], wq_sb[:, k, :], start=(k == 0), stop=(k == KC - 1))
            m.then_inc(u_done, 1)

            def transpose_a(g, j):
                pe.wait_ge(a_ready, TJ * g + j + 1)
                chunks4(tp[a_tp[j]], lambda k: a_sb[:, j, k * P:(k + 1) * P], aT_done)

            def product_g(g, c, first):
                if not first or c >= 2:
                    pe.wait_ge(g_evac, KC * g + c - 1)
                cc = slice(c * P, (c + 1) * P)
                product3(gb[c % 2][:, 0:GT], KC, lambda k: m_hi[:, k, cc], lambda k: m_lo[:, k, cc],
                         lambda k: aT_hi[:, k, :], lambda k: aT_lo[:, k, :]).then_inc(g_done, 1)

            pe.wait_ge(ident_done, 1)
            for j in range(TJ):
                transpose_a(0, j)
            pe.wait_ge(bias_in, 32)
            for k in range(KC):
                nc.tensor.matmul(bb_ps, bk_rows[:, k, :], bqk[:, 0, k:k + 1], start=(k == 0), stop=(k == KC - 1))
            for c in range(KC):
                for k in range(KC):
                    m = nc.tensor.matmul(w_ps[:, c:c + 1], wk_sb[:, k, c * P:(c + 1) * P], bqk[:, 0, k:k + 1],
                                         start=(k == 0), stop=(k == KC - 1))
            m.then_inc(vec_done, 1)
            pe.wait_ge(m_lo_done, KC)
            pe.wait_ge(aT_lo_done, TJ)
            for c in range(KC - 1):
                product_g(0, c, True)

            def transpose_h(g, banks):
                for j in range(TJ):
                    pe.wait_ge(h_ready, TJ * g + j + 1)
                    chunks4(banks[j], lambda k: h_sb[:, j, k * P:(k + 1) * P], hT_done)

            def logits(g, first):
                pe.wait_ge(hT_evac, TJ * g + TJ)
                if not first:
                    pe.wait_ge(ranks_read, g)
                for j in range(TJ):
                    for k in range(KC):
                        m = nc.tensor.matmul(l_ps[:, j], hT[:, j, k, :], wg_sb[:, k, :], start=(k == 0), stop=(k == KC - 1))
                m.then_inc(logits_done, 1)

            def ranks(g):
                pe.wait_ge(mask_ready, g + 1)
                pe.wait_ge(logits_read, g + 1)
                nc.tensor.matmul(rk_ps[:, 0], earlier[:, :], mask[:, 0], start=True, stop=False)
                nc.tensor.matmul(rk_ps[:, 0], ones_b[:, :], taken[:, :], start=False, stop=True)
                nc.tensor.matmul(rk_ps[:, 1], earlier[:, :], mask[:, 1], start=True, stop=False)
                nc.tensor.matmul(rk_ps[:, 1], ones_b[:, :], mask[:, 0], start=False, stop=False)
                return nc.tensor.matmul(rk_ps[:, 1], ones_b[:, :], taken[:, :], start=False, stop=True)

            def counts(g, read):
                pe.wait_ge(logits_read, read)
                pe.wait_ge(ranks_read, read)
                pe.wait_ge(mask_step, MS * (g + 1) + 1)
                nc.tensor.matmul(cnt_full_ps, ones_b[:, :], taken[:, :], start=True, stop=True).then_inc(count_done, 1)

            def transpose_c(parity, j):
                chunks4(tp[c_tp[j]], lambda k: c_sb[:, parity, j, k * P:(k + 1) * P], cT_done)

            def scores(g, first):
                pe.wait_ge(g_evac, KC * g + KC)
                for j in range(TJ):
                    pe.wait_ge(cT_evac, TJ * g + j + 1)
                    if not first:
                        pe.wait_ge(x1_ready, TJ * (g - 1) + j + 1)
                    for k in range(KC):
                        m = nc.tensor.matmul(sc[j][:, 0:P], gT[:, k, j * P:(j + 1) * P], cT[:, j, k, :],
                                             start=(k == 0), stop=(k == KC - 1))
                    m.then_inc(scores_done, 1)

            def transpose_p(g):
                for j in range(TJ):
                    pe.wait_ge(exp_done, TJ * g + j + 1)
                    nc.tensor.transpose(sc[j][:, P:2 * P], p_sb[:, j], ident[:, :]).then_inc(pt_done, 1)

            def attend(g, parity, j):
                pe.wait_ge(pt_evac, TJ * g + j + 1)
                nc.tensor.matmul(sc[j][:, :], p_sb[:, j], c_sb[:, parity, j, :], start=True, stop=True).then_inc(pv_done, 1)

            def group(g, parity, first, ahead, second=False):
                if isinstance(g, int) and g == AHEAD + 1:
                    counts(AHEAD - 1, AHEAD)
                scores(g, first)
                pe.wait_ge(aT_lo_done, TJ * (g + 1) + TJ)
                for c in range(KC - 1):
                    product_g(g + 1, c, False)
                if not first:
                    transpose_h(g - 1, former_h)
                product_g(g + 1, KC - 1, False)
                if not first:
                    if isinstance(g, int) and g == AHEAD + 1:
                        pe.wait_ge(route_step, 1)
                    logits(g - 1, second)
                transpose_p(g)
                if ahead:
                    for j in range(TJ):
                        transpose_a(g + 2, j)
                pe.wait_ge(c_in, 16 * (g + 1))
                if not first:
                    pe.wait_ge(hT_evac, TJ * (g - 1) + 1)
                transpose_c(1 - parity, 0)
                if not first:
                    ranks(g - 1).then_inc(ranks_done, 1)
                attend(g, parity, 0)
                if ahead:
                    pe.wait_ge(aT_lo_done, TJ * (g + 2) + 1)
                transpose_c(1 - parity, 1)
                attend(g, parity, 1)

            pe.wait_ge(c_first, 16)
            pe.wait_ge(vec_evac, 1)
            for j in range(TJ):
                transpose_c(0, j)
            product_g(0, KC - 1, True)
            pe.wait_ge(cT_evac, TJ)
            for j in range(TJ):
                transpose_a(1, j)
            pe.wait_ge(small_in, 64)
            group(0, 0, True, True)
            group(1, 1, False, True, second=True)
            with pe.Fori(1, GROUPS // 2 - 1) as i:
                for parity in range(2):
                    group(2 * i + parity, parity, False, True)
            group(GROUPS - 2, 0, False, False)

            def transpose_rows(b, u, arrived):
                pe.wait_ge(row_in[u], arrived)
                chunks4(tb[u % XU], lambda k: rows[:, u, k * P:(k + 1) * P], xT_done)

            def block_product(b, u, first):
                e = pe.value_load(expert_of[0:1, ds(b, 1)], min_val=0, max_val=E - 1)
                pe.wait_ge(xT_lo_done, b + 1)
                if isinstance(b, int) and 2 <= b < 2 * BU:
                    pe.wait_ge(y_biased, b - 1)
                elif not first:
                    pe.wait_ge(y_biased, b - BU + 1)
                product3(yb_of(b, u)[:, :], KC, lambda k: xT_hi[:, u % XU, k, :], lambda k: xT_lo[:, u % XU, k, :],
                         lambda k: we_hi[:, ds(e * KC + k, 1), :], lambda k: we_lo[:, ds(e * KC + k, 1), :]).then_inc(y_done, 1)

            def turn_rows(b):
                transpose_rows(b, b % BU, 16 * (b // BU) + 16)

            def turn_product(b):
                block_product(b, b % BU, b < BU)

            g = GROUPS - 1
            scores(g, False)
            turn_rows(0)
            pe.wait_ge(lists_known, 2)
            pe.wait_ge(w_lo_done, E * KC)
            turn_product(0)
            transpose_h(g - 1, former_h)
            turn_rows(1)
            transpose_p(g)
            logits(g - 1, False)
            for j in range(TJ):
                attend(g, 1, j)
            turn_product(1)
            ranks(g - 1).then_inc(ranks_done, 1)
            turn_rows(2)
            turn_rows(3)
            turn_product(2)
            transpose_h(g, last_h)
            turn_rows(4)
            turn_product(3)
            logits(g, False)
            turn_rows(5)
            turn_product(4)
            ranks(g).then_inc(ranks_done, 1)
            turn_rows(6)
            turn_product(5)
            counts(g, GROUPS)
            turn_rows(7)
            turn_product(6)
            turn_rows(8)
            turn_product(7)
            for b in range(2 * BU, EARLY):
                turn_rows(b + 1)
                turn_product(b)
            pe.wait_ge(lists_known, 4)
            with pe.Fori(EARLY // BU, TURNS) as i:
                for u in range(BU):
                    transpose_rows(i * BU + u + 1, (u + 1) % BU, 16 * i + 16 * ((u + 1) // BU) + 16)
                    block_product(i * BU + u, u, False)
            for b in range(TURNS * BU, BLOCKS):
                if b + 1 < BLOCKS:
                    transpose_rows(b + 1, (b + 1) % BU, 16 * ((b + 1) // BU) + 16)
                block_product(b, b % BU, False)


_INS = ["x", "ctx_4096", "g_xattn", "g_ffn", "L0_xattn_Wq", "L0_xattn_bq", "L0_xattn_Wk", "L0_xattn_bk",
        "L0_ffn_W_gate", "L0_ffn_b_gate", "L0_ffn_W_e", "L0_ffn_b_e"]


def kernel(**inputs):
    import numpy as _np
    import concourse.bacc as _bacc
    from concourse import mybir as _mybir
    from concourse.bass_utils import run_bass_kernel_spmd as _run

    nc = _bacc.Bacc("TRN2", target_bir_lowering=False, num_devices=1)
    arrays, args = {}, []
    for name in _INS:
        a = _np.ascontiguousarray(inputs[name])
        arrays[f"in_{name}"] = a
        args.append(nc.dram_tensor(f"in_{name}", a.shape, _mybir.dt.from_np(a.dtype), kind="ExternalInput").ap())
    out = nc.dram_tensor("out_rows", (N + PADS, D), _mybir.dt.float32, kind="ExternalOutput").ap()
    gated_xattn_moe(nc, *args, out)
    r = _run(nc, [arrays], core_ids=[0])
    return _np.asarray(r.results[0]["out_rows"])[:N].reshape(B, S, D)
```
